# Optimizing a Trainium2 kernel written in Bass

```python
import numpy as np
import jax
import jax.numpy as jnp

def _softmax(x, axis=-1):
    return jax.nn.softmax(x, axis=axis)

def _gelu(x):
    return jax.nn.gelu(x, approximate=True)

def _silu(x):
    return jax.nn.silu(x)

def _sigmoid(x):
    return jax.nn.sigmoid(x)

def _layernorm(x, axis=-1, eps=1e-05):
    m = jnp.mean(x, axis=axis, keepdims=True)
    v = jnp.var(x, axis=axis, keepdims=True)
    return (x - m) / jnp.sqrt(v + eps)

def _scatter_add(tgt, idx, src, axis=0):
    return tgt.at[idx].add(src)

def _segment_sum(src, seg, n):
    return jax.ops.segment_sum(src, seg, n)
kernel_name = 'mk_vit_tower_cls_d1_tok_img768_r4_64a31e'

def setup_inputs(seed: int=0):
    np.random.seed(seed)
    _w = jnp.asarray

    def _rec_inputs():
        import jax
        import jax.numpy as jnp
        _rk = jax.random.key(seed)
        x = 1.64766e-05 + 1.00005 * jax.random.normal(jax.random.fold_in(_rk, 1), (4, 3, 512, 192), jnp.float32)
        cls_tok = 0.02 * jax.random.normal(jax.random.fold_in(_rk, 5), (1, 1, 192), jnp.float32)
        return (x, cls_tok)
    x, cls_tok = _rec_inputs()

    def _L0_tok_setup():
        import jax, jax.numpy as jnp
        import numpy as np
        NUM_BANDS = 6
        D_MODEL = 192
        B, N = (2, 512)
        IN_FEATURES = 3 * NUM_BANDS * 2 * D_MODEL
        key = jax.random.key(seed)
        k_xyz, k_w = jax.random.split(key)
        xyz = jax.random.normal(k_xyz, (B, 3, N, D_MODEL), dtype=jnp.float32)
        freq_bands = 2.0 ** jnp.linspace(0.0, NUM_BANDS - 1, NUM_BANDS).astype(jnp.float32)
        bound = 1.0 / np.sqrt(IN_FEATURES)
        W = jax.random.uniform(k_w, (D_MODEL, IN_FEATURES), dtype=jnp.float32, minval=-bound, maxval=bound)
        return {'xyz': xyz, 'freq_bands': freq_bands, 'W': W}
    _L0_tok_all = _L0_tok_setup()
    _L0_tok_in = {k: v for k, v in _L0_tok_all.items() if k in ('freq_bands', 'W')}
    del _L0_tok_all

    def _L0_attn_setup():
        import jax, jax.numpy as jnp
        import numpy as np
        B, L, D, M = (1, 512, 192, 64)
        key = jax.random.key(seed)
        ks = jax.random.split(key, 9)

        def w(k, shape):
            return jax.random.normal(k, shape, jnp.float32) * shape[0] ** (-0.5)
        x = jax.random.normal(ks[0], (B, L, D), jnp.float32)
        Wq = w(ks[1], (D, M))
        Wk = w(ks[2], (D, M))
        Wv = w(ks[3], (D, D))
        Wf = w(ks[4], (D, M))
        bf = jnp.zeros((M,), jnp.float32)
        Wo = w(ks[5], (D, D))
        gamma = jnp.ones((D,), jnp.float32)
        beta = jnp.zeros((D,), jnp.float32)
        return {'x': x, 'Wq': Wq, 'Wk': Wk, 'Wv': Wv, 'Wf': Wf, 'bf': bf, 'Wo': Wo, 'gamma': gamma, 'beta': beta}
    _L0_attn_all = _L0_attn_setup()
    _L0_attn_in = {k: v for k, v in _L0_attn_all.items() if k in ('Wq', 'Wk', 'Wv', 'Wf', 'bf', 'Wo', 'gamma', 'beta')}
    del _L0_attn_all

    def _L0_ffn_setup():
        import jax, jax.numpy as jnp
        import numpy as np
        B, S, D = (4, 256, 192)
        E = 8
        H = 192
        HS = 768
        TOPK_ROUTED = 2
        key = jax.random.key(seed)
        ks = jax.random.split(key, 10)
        w = lambda k, shape: jax.random.normal(k, shape, dtype=jnp.float32) * 0.02
        return {'x': jax.random.normal(ks[0], (B, S, D), dtype=jnp.float32), 'router_w': w(ks[1], (D, E)), 'w_gate': w(ks[2], (E, D, H)), 'w_up': w(ks[3], (E, D, H)), 'w_down': w(ks[4], (E, H, D)), 'ws_gate': w(ks[5], (D, HS)), 'ws_up': w(ks[6], (D, HS)), 'ws_down': w(ks[7], (HS, D)), 'sg_w': w(ks[8], (D, 1)), 'sg_b': jnp.zeros((1,), jnp.float32)}
    _L0_ffn_all = _L0_ffn_setup()
    _L0_ffn_in = {k: v for k, v in _L0_ffn_all.items() if k in ('router_w', 'w_gate', 'w_up', 'w_down', 'ws_gate', 'ws_up', 'ws_down', 'sg_w', 'sg_b')}
    del _L0_ffn_all
    return {'x': x, 'cls_tok': cls_tok, 'L0_tok_freq_bands': _L0_tok_in['freq_bands'], 'L0_tok_W': _L0_tok_in['W'], 'L0_attn_Wq': _L0_attn_in['Wq'], 'L0_attn_Wk': _L0_attn_in['Wk'], 'L0_attn_Wv': _L0_attn_in['Wv'], 'L0_attn_Wf': _L0_attn_in['Wf'], 'L0_attn_bf': _L0_attn_in['bf'], 'L0_attn_Wo': _L0_attn_in['Wo'], 'L0_attn_gamma': _L0_attn_in['gamma'], 'L0_attn_beta': _L0_attn_in['beta'], 'L0_ffn_router_w': _L0_ffn_in['router_w'], 'L0_ffn_w_gate': _L0_ffn_in['w_gate'], 'L0_ffn_w_up': _L0_ffn_in['w_up'], 'L0_ffn_w_down': _L0_ffn_in['w_down'], 'L0_ffn_ws_gate': _L0_ffn_in['ws_gate'], 'L0_ffn_ws_up': _L0_ffn_in['ws_up'], 'L0_ffn_ws_down': _L0_ffn_in['ws_down'], 'L0_ffn_sg_w': _L0_ffn_in['sg_w'], 'L0_ffn_sg_b': _L0_ffn_in['sg_b']}

def reference(x, cls_tok, L0_tok_freq_bands, L0_tok_W, L0_attn_Wq, L0_attn_Wk, L0_attn_Wv, L0_attn_Wf, L0_attn_bf, L0_attn_Wo, L0_attn_gamma, L0_attn_beta, L0_ffn_router_w, L0_ffn_w_gate, L0_ffn_w_up, L0_ffn_w_down, L0_ffn_ws_gate, L0_ffn_ws_up, L0_ffn_ws_down, L0_ffn_sg_w, L0_ffn_sg_b):
    import jax
    import jax.numpy as jnp

    def _L0_tok_ref(xyz, freq_bands, W):
        import jax, jax.numpy as jnp
        import numpy as np
        NUM_BANDS = 6
        D_MODEL = 192
        B, N = (2, 512)
        IN_FEATURES = 3 * NUM_BANDS * 2 * D_MODEL
        b, c, n, d = xyz.shape
        xb = 2.0 * jnp.pi * xyz[..., None] * freq_bands
        feat = jnp.concatenate([jnp.sin(xb), jnp.cos(xb)], axis=-1)
        feat = feat.reshape(b, n, -1)
        return jnp.einsum('bnf,of->bno', feat, W)

    def _L0_attn_ref(x, Wq, Wk, Wv, Wf, bf, Wo, gamma, beta):
        import jax, jax.numpy as jnp
        import numpy as np
        B, L, D, M = (1, 512, 192, 64)
        m_dim = Wq.shape[1]
        scale = m_dim ** (-0.5)
        q = (jax.nn.elu(x @ Wq) + 1.0) * scale
        k = jax.nn.elu(x @ Wk) + 1.0
        v = x @ Wv
        forget = jax.nn.sigmoid(x @ Wf + bf)
        log_f = jnp.log(jnp.clip(forget, 1e-06, None))
        log_f_cum = jnp.clip(jnp.cumsum(log_f, axis=1), -20.0, 20.0)
        exp_neg = jnp.exp(-log_f_cum)
        exp_pos = jnp.exp(log_f_cum)
        kv = k[..., :, None] * v[..., None, :]
        cum_kv = jnp.cumsum(exp_neg[..., None] * kv, axis=1)
        Mstate = exp_pos[..., None] * cum_kv
        z = exp_pos * jnp.cumsum(exp_neg * k, axis=1)
        numerator = jnp.einsum('blm,blmd->bld', q, Mstate)
        denominator = jnp.einsum('blm,blm->bl', q, z)[..., None] + 1e-06
        h = numerator / denominator
        mu = jnp.mean(h, axis=-1, keepdims=True)
        var = jnp.var(h, axis=-1, keepdims=True)
        normed = (h - mu) / jnp.sqrt(var + 1e-05) * gamma + beta
        return normed @ Wo

    def _L0_ffn_ref(x, router_w, w_gate, w_up, w_down, ws_gate, ws_up, ws_down, sg_w, sg_b):
        import jax, jax.numpy as jnp
        import numpy as np
        B, S, D = (4, 256, 192)
        E = 8
        H = 192
        HS = 768
        TOPK_ROUTED = 2
        probs = jax.nn.softmax(x @ router_w, axis=-1)
        gates, idx = jax.lax.top_k(probs, TOPK_ROUTED)
        gates = gates / jnp.sum(gates, axis=-1, keepdims=True)
        n_exp = router_w.shape[1]
        dense_g = jnp.sum(jax.nn.one_hot(idx, n_exp, dtype=x.dtype) * gates[..., None], axis=-2)
        g = jax.nn.silu(jnp.einsum('bsd,edh->bseh', x, w_gate))
        u = jnp.einsum('bsd,edh->bseh', x, w_up)
        expert_out = jnp.einsum('bseh,ehd->bsed', g * u, w_down)
        routed = jnp.einsum('bse,bsed->bsd', dense_g, expert_out)
        shared = jax.nn.silu(x @ ws_gate) * (x @ ws_up) @ ws_down
        alpha = jax.nn.sigmoid(x @ sg_w + sg_b)
        return alpha * shared + (1.0 - alpha) * routed
    h = _L0_tok_ref(x, L0_tok_freq_bands, L0_tok_W)
    h = jnp.concatenate([jnp.broadcast_to(cls_tok, (h.shape[0], 1, h.shape[2])), h], axis=1)
    h = h + _L0_attn_ref(_layernorm(h, axis=-1), L0_attn_Wq, L0_attn_Wk, L0_attn_Wv, L0_attn_Wf, L0_attn_bf, L0_attn_Wo, L0_attn_gamma, L0_attn_beta)
    h = h + _L0_ffn_ref(_layernorm(h, axis=-1), L0_ffn_router_w, L0_ffn_w_gate, L0_ffn_w_up, L0_ffn_w_down, L0_ffn_ws_gate, L0_ffn_ws_up, L0_ffn_ws_down, L0_ffn_sg_w, L0_ffn_sg_b)
    return h

_drawn_inputs = setup_inputs


def setup_inputs(seed=0):
    import zlib

    import numpy as np

    out = dict(_drawn_inputs(seed))
    spreads = {'L0_attn_bf': (0.0, 0.546), 'L0_attn_gamma': (1.0, 0.2), 'L0_attn_beta': (0.0, 0.1)}
    factors = {'L0_attn_Wf': 3.137,
     'L0_ffn_router_w': 8.0,
     'L0_ffn_w_gate': 8.0,
     'L0_ffn_w_up': 8.0,
     'L0_ffn_w_down': 8.0,
     'L0_ffn_ws_gate': 5.451,
     'L0_ffn_ws_up': 5.468,
     'L0_ffn_ws_down': 5.351,
     'L0_ffn_sg_w': 8.0}
    for name, (base, spread) in spreads.items():
        noise = np.random.default_rng([zlib.crc32(name.encode()), seed]).standard_normal(out[name].shape)
        drawn = base * np.exp(spread * noise) if base else spread * noise
        out[name] = jnp.asarray(drawn.astype(out[name].dtype))
    for name, factor in factors.items():
        out[name] = (out[name] * factor).astype(out[name].dtype)
    return out
```

```python
from contextlib import ExitStack

import numpy as np

import concourse.bass as bass
from concourse import mybir

F32 = mybir.dt.float32
F32R = mybir.dt.float32r
I32 = mybir.dt.int32
ALU = mybir.AluOpType
ACT = mybir.ActivationFunctionType
AX_X = mybir.AxisListType.X

P = 128
B = 4
C3 = 3
T = 512
D = 192
DB = D - P
NF = 6
M = 64
NE = 8
HS = 768
HID = HS + NE * D
NC = HID // P
NCS = HS // P
NT = T // P
J = C3 * D
JC = J // P
NG = 2 * JC + 1
SLOTS = 3
CLS = 2
NR = NE + 2
GLO = 32
GR = GLO + NE + 1
PIECES = 6
PC = NC // PIECES
LNS = 14
MAGIC = 1.5 * 2.0 ** 23
RSQRT_SEED = float(0x5F3759DF)
TWO_PI = float(np.float32(2.0 * np.pi))
HALF_PI = float(np.float32(0.5 * np.pi))
LN_EPS = 1e-5
DEN_EPS = 1e-6
MAX_ODDS = float(np.float32(1e6) - np.float32(1.0))
CLIP = 20.0
FAR = 1e30


def build(nc, xT, wT, freqs, cls_tok, wq, wk, wv, wf, bf, gamma, beta, wo,
          wr, sg_w, sg_b, wgu, wd, consts, out):
    with ExitStack() as ctx:
        def sb(name, shape, dt=F32):
            return ctx.enter_context(nc.sbuf_tensor(name, shape, dt))

        def sem(name):
            return ctx.enter_context(nc.semaphore(name))

        w_tok = sb("w_tok", [P, NG, 2 * 3, D])
        wa_hi = sb("wa_hi", [P, NC, 2, P], F32R)
        wa_lo = sb("wa_lo", [P, NC, 2, P], F32R)
        wb = sb("wb", [P, NC, 2, P], F32R)
        w_down = sb("w_down", [P, NC, D])
        wqk_a, wqk_b = sb("wqk_a", [P, 2, M]), sb("wqk_b", [P, 2, M])[DB:P]
        wff_a, wff_b = sb("wff_a", [P, 2, M]), sb("wff_b", [P, 2, M])[DB:P]
        wv_a, wv_b = sb("wv_a", [P, D]), sb("wv_b", [P, D])[DB:P]
        wo_a, wo_b = sb("wo_a", [P, D]), sb("wo_b", [P, D])[DB:P]
        gb_a, gb_b = sb("gb_a", [P, 2]), sb("gb_b", [DB, 2])
        neg_bf = sb("neg_bf", [P, 1])
        wr_raw = sb("wr_raw", [P, 2, NR])
        wra_hi, wra_lo, wrb = (sb(n, [P, NR], F32R) for n in ("wra_hi", "wra_lo", "wrb"))
        sgb = sb("sgb", [P, 1])
        f_col = sb("f_col", [P, NF + 3])
        ident, causal = sb("ident", [P, P]), sb("causal", [P, P])
        qk_scale, p_sign = sb("qk_scale", [P, 1]), sb("p_sign", [P, 1])
        half_pi = sb("half_pi", [P, 1])
        rank = sb("rank", [P, NE])
        pick_raw = sb("pick_raw", [GR, NE + 1])
        pick = sb("pick", [GR, NE + 1, P // 2], F32R)
        one = sb("one", [P, 1])
        x = sb("x", [P, JC + 1, T])
        feat = sb("feat", [P, SLOTS, 6, T])
        h, h2 = sb("h", [P, NT, D]), sb("h2", [P, NT, D])
        xn = sb("xn", [P, NT, D + DB])
        xt_a = sb("xt_a", [P, T])
        v = sb("v", [P, NT, D + 1])
        r = sb("r", [P, 7, T])
        xh_a, xl_a = sb("xh_a", [P, T], F32R), sb("xl_a", [P, T], F32R)
        xh_b, xl_b = sb("xh_b", [P, T], F32R), sb("xl_b", [DB, T], F32R)
        gate_t = sb("gate_t", [GR, T], F32R)
        h_c, xn_c = h[0:CLS, 0:1, :], xn[0:CLS, 0:1, :]
        h2_c = sb("h2_c", [CLS, 1, D])
        k_c, v_c = sb("k_c", [M, CLS]), sb("v_c", [CLS, D + 1])
        s_c = sb("s_c", [P, 1])
        xhc_a, xlc_a = sb("xhc_a", [P, CLS], F32R), sb("xlc_a", [P, CLS], F32R)
        xhc_b, xlc_b = sb("xhc_b", [P, CLS], F32R), sb("xlc_b", [DB, CLS], F32R)
        gatec_t = sb("gatec_t", [GR, CLS], F32R)
        act_c = sb("act_c", [P, 7, CLS])
        st, mv = sb("st", [P, NT, 6]), sb("mv", [P, NT, 2])
        ve, y, ya = sb("ve", [P, NT]), sb("y", [P, NT]), sb("ya", [P, NT])
        den, rden = sb("den", [P, NT]), sb("rden", [P, NT])
        lg, lg2 = sb("lg", [P, NT, NE + 1]), sb("lg2", [P, NT, NE])
        top = sb("top", [P, 4, NT])
        oh1, oh2, key = sb("oh1", [P, NT, NE]), sb("oh2", [P, NT, NE]), sb("key", [P, NT, NE])
        dz, ez, iz = sb("dz", [P, NT, 2]), sb("ez", [P, NT, 2]), sb("iz", [P, NT, 2])
        ga = sb("ga", [P, NT, 3])
        gm = sb("gm", [P, NT, NE + 1])
        gm_hi = sb("gm_hi", [P, NT, NE + 1], F32R)
        gt = sb("gt", [P, NT, GR])

        ps = ctx.enter_context(nc.psum_tensor("ps", [P, 8, 512], F32))
        TB0, DN0, PB0 = 0, 2, 4

        R_E, R_PHI, R_S, R_P, R_C, R_QK, R_K = range(7)
        at = r[:, 0:4, :]
        xt_b = r[DB:P, R_K, :]

        names = """w_small f_in wgu_raw wdown_in cls_in split_hi split_done router_hi router_split consts_ok
            n_raw n_ready r_raw r_ready sin_ready tok_group
            h_ready ln_step xn_ready xpose1 xta_ready xtb_ready qk_psum f_psum v_psum v_ready
            e_ready ee_ready odds_ready oddsc_ready s_ready scan_ready c_ready p_ready phi_ready
            qk_ready k_in at_psum at_diag at_rest av_psum den_ready rden_ready hh_ready hn_ready
            xpose2 nta_ready ntb_ready wo_psum h2_ready xn2_ready xpose3 xh_ready xl_ready
            lg_psum top_step dz_ready ez_ready gt_step gt_psum gate_ready
            g_psum u_psum m_psum silu_ready t_ready hid_ready down_ready out_ready out_dma clsout_dma"""
        S = {n: sem(n) for n in names.split()}
        (w_small, f_in, wgu_raw, wdown_in, cls_in, split_hi, split_done, router_hi, router_split, consts_ok,
         n_raw, n_ready, r_raw, r_ready, sin_ready, tok_group,
         h_ready, ln_step, xn_ready, xpose1, xta_ready, xtb_ready, qk_psum, f_psum, v_psum, v_ready,
         e_ready, ee_ready, odds_ready, oddsc_ready, s_ready, scan_ready, c_ready, p_ready, phi_ready,
         qk_ready, k_in, at_psum, at_diag, at_rest, av_psum, den_ready, rden_ready, hh_ready, hn_ready,
         xpose2, nta_ready, ntb_ready, wo_psum, h2_ready, xn2_ready, xpose3, xh_ready, xl_ready,
         lg_psum, top_step, dz_ready, ez_ready, gt_step, gt_psum, gate_ready,
         g_psum, u_psum, m_psum, silu_ready, t_ready, hid_ready, down_ready, out_ready, out_dma,
         clsout_dma) = (S[n] for n in names.split())
        wt_in = [sem(f"wt_in{k}") for k in range(NG)]
        xc_in = [sem(f"xc_in{k}") for k in range(JC + 1)]
        N_SMALL = 23

        def width(a):
            cls = isinstance(a, int) and a == 0
            return (CLS, CLS, 1) if cls else (T, P, NT)

        def tiles(a):
            if isinstance(a, int) and a == 0:
                return h_c, h2_c, xn_c, xhc_a, xlc_a, xhc_b, xlc_b, gatec_t
            return h, h2, xn, xh_a, xl_a, xh_b, xl_b, gate_t

        def x_block(k):
            return k // 2 if k < 2 * JC else JC

        def x_parts(k):
            return 16 if k < 2 * JC else 32

        def f_index(k, i):
            return 3 * (k % 2) + i if k < 2 * JC else NF + i

        block = ctx.enter_context(nc.Block())

        @block.sync
        def _(sp):
            def small(dst, src):
                sp.dma_start(dst, src).then_inc(w_small, 16)

            def load_x(b, k):
                sem_ = xc_in[k]
                if k < JC:
                    sp.dma_start(x[:, k, :], xT[b, k * P:(k + 1) * P, :]).then_inc(sem_, 16)
                else:
                    for half in range(2):
                        sp.dma_start(x[half * DB:(half + 1) * DB, k, :], xT[b, JC * P:J, :]).then_inc(sem_, 16)

            def load_wt(k):
                if k < 2 * JC:
                    j0 = (k // 2) * P
                    src = wT[j0:j0 + P, :, :].rearrange("j (c q i) o -> j c q (i o)", c=2, q=2)[:, :, k % 2, :]
                    sp.dma_start(w_tok[:, k, :, :].rearrange("p (c i) o -> p c (i o)", c=2), src).then_inc(wt_in[k], 16)
                else:
                    for half in range(2):
                        src = wT[JC * P:J, :, :].rearrange("j (c f) o -> j c f o", f=2)[:, :, half, :]
                        sp.dma_start(w_tok[half * DB:(half + 1) * DB, k, :, :], src).then_inc(wt_in[k], 16)

            for half in range(2):
                sp.dma_start(f_col[half * DB:(half + 1) * DB, :],
                             freqs[half:half + 1, :].to_broadcast([DB, NF + 3])).then_inc(f_in, 16)
            load_x(0, 0)
            sp.dma_start(h_c[:, 0, :], cls_tok[0:1, :].to_broadcast([CLS, D])).then_inc(cls_in, 16)
            small(ident[:, :], consts[:, 0:P])
            small(wqk_a[:, 0, :], wq[0:P, :])
            small(wqk_a[:, 1, :], wk[0:P, :])
            small(wqk_b[:, 0, :], wq[P:D, :])
            small(wqk_b[:, 1, :], wk[P:D, :])
            for i in range(2):
                small(wff_a[:, i, :], wf[0:P, :])
                small(wff_b[:, i, :], wf[P:D, :])
                small(neg_bf[i * M:(i + 1) * M, :], bf)
            small(wv_a[:, :], wv[0:P, :])
            small(wv_b[:, :], wv[P:D, :])
            load_wt(0)
            small(wo_a[:, :], wo[0:P, :])
            small(wo_b[:, :], wo[P:D, :])
            for i, src in enumerate((gamma, beta)):
                small(gb_a[:, i:i + 1], src[0:P, :])
                small(gb_b[:, i:i + 1], src[P:D, :])
            small(causal[:, :], consts[:, P:2 * P])
            small(sgb[:, :], sg_b[0:1, :].to_broadcast([P, 1]))
            sp.dma_start(pick_raw[:, :], consts[0:GR, 2 * P:2 * P + NE + 1]).then_inc(w_small, 16)
            sp.dma_start(rank[:, :], consts[:, 2 * P + NE + 1:2 * P + 2 * NE + 1]).then_inc(w_small, 16)
            sp.wait_ge(consts_ok, 1)
            for lo, hi, half, row in ((0, P, 0, 0), (0, DB, 1, P), (DB, P, 1, P)):
                sp.dma_start(wr_raw[lo:hi, half, 0:NE], wr[row:row + hi - lo, :]).then_inc(router_hi, 16)
                sp.dma_start(wr_raw[lo:hi, half, NE:NE + 1], sg_w[row:row + hi - lo, :]).then_inc(router_hi, 16)

            def load_piece(p):
                if p >= 1:
                    sp.wait_ge(split_done, 2 * p)
                else:
                    sp.wait_ge(xpose3, 1)
                cut = slice(PC * p, PC * (p + 1))
                sp.dma_start(h2[:, :, :].rearrange("p a b -> p (a b)"),
                             wgu[0:P, cut, :].rearrange("k c n -> k (c n)")).then_inc(wgu_raw, 16)
                for half in range(2):
                    sp.dma_start(xn[half * DB:(half + 1) * DB, :, :].rearrange("p a b -> p (a b)")[:, 0:PC * 2 * P],
                                 wgu[P:D, cut, :].rearrange("k c n -> k (c n)")).then_inc(wgu_raw, 16)

            for k in range(1, NG):
                if k % 2 == 0:
                    load_x(0, x_block(k))
                load_wt(k)
                if k >= 3:
                    load_piece(k - 3)
            sp.dma_start(w_down[:, :, :], wd.rearrange("(c p) d -> p c d", p=P)).then_inc(wdown_in, 16)

            def next_x(a):
                sp.wait_ge(r_ready, NG * (a + 1))
                for k in range(JC + 1):
                    load_x(a + 1, k)

            def store(b, f):
                sp.wait_ge(out_ready, f + 1)
                sp.dma_start(out[b, 1:T + 1, :].rearrange("(i p) d -> p i d", p=P), h2[:, :, :]).then_inc(out_dma, 16)

            def body(a):
                next_x(a)
                store(a - 1, a - 1)

            next_x(0)
            for a in range(1, B - 1):
                body(a)
            store(B - 2, B - 2)
            sp.wait_ge(out_ready, B)
            for b in range(B):
                sp.dma_start(out[b, 0:1, :], h2_c[0:1, 0, :]).then_inc(clsout_dma, 16)
            store(B - 1, B)
            sp.wait_ge(out_dma, 16 * B)
            sp.wait_ge(clsout_dma, 16 * B)

        @block.gpsimd
        def _(pool):
            def rounds(a, k):
                q = NG * a + k
                if not (isinstance(a, int) and q < SLOTS):
                    pool.wait_ge(tok_group, q - SLOTS + 1)
                if isinstance(a, int) and a == 0 and k == 0:
                    pool.wait_ge(f_in, 32)
                pool.wait_ge(xc_in[x_block(k)], x_parts(k) * (a + 1))
                for i in range(3):
                    fi = f_index(k, i)
                    ins = pool.tensor_scalar(feat[:, k % SLOTS, i, :], x[:, x_block(k), :], f_col[:, fi:fi + 1],
                                             MAGIC, ALU.mult, ALU.add)
                ins.then_inc(n_raw, 1)
                pool.wait_ge(n_raw, q + 1)
                pool.tensor_scalar(feat[:, k % SLOTS, 0:3, :], feat[:, k % SLOTS, 0:3, :], -MAGIC, 1.0,
                                   ALU.add, ALU.mult).then_inc(n_ready, 1)

            for a in range(B):
                for k in range(NG):
                    rounds(a, k)

        @block.scalar
        def _(act):
            def sines(a, k):
                q = NG * a + k
                act.wait_ge(r_ready, q + 1)
                act.activation(feat[:, k % SLOTS, 0:3, :], feat[:, k % SLOTS, 0:3, :], ACT.Sin, scale=TWO_PI)
                act.activation(feat[:, k % SLOTS, 3:6, :], feat[:, k % SLOTS, 3:6, :], ACT.Sin,
                               bias=half_pi[:, :], scale=-TWO_PI).then_inc(sin_ready, 1)

            def take_h(b):
                act.wait_ge(tok_group, NG * (b + 1))
                act.wait_ge(h2_ready, b + 1)
                for i in range(2):
                    ins = act.activation(h[:, 2 * i:2 * i + 2, :].rearrange("p a b -> p (a b)"),
                                         ps[:, TB0 + i, 0:2 * D], ACT.Copy)
                ins.then_inc(h_ready, 1)

            def attn1(a):
                W, TP, nt = width(a)
                act.wait_ge(xpose1, a + 1)
                act.activation(xt_a[:, 0:W], ps[:, PB0, 0:W], ACT.Copy).then_inc(xta_ready, 1)

            def attn2(a):
                W, TP, nt = width(a)
                act.wait_ge(v_psum, a + 1)
                for i in range((nt + 1) // 2):
                    n = min(2, nt)
                    ins = act.activation(v[0:TP, 2 * i:2 * i + n, 0:D],
                                         ps[0:TP, DN0 + i, 0:n * D].rearrange("p (t d) -> p t d", d=D), ACT.Copy)
                ins.then_inc(v_ready, 1)
                if not (isinstance(a, int) and a < 2):
                    act.wait_ge(out_ready, a - 1)
                    act.wait_ge(down_ready, NC * (a - 1))
                act.wait_ge(f_psum, a + 1)
                act.activation(r[:, R_S, 0:W], ps[:, PB0 + 3, 0:W], ACT.Exp, bias=neg_bf[:, :],
                               scale=-1.0).then_inc(odds_ready, 1)
                act.wait_ge(e_ready, a + 1)
                act.activation(r[:, R_E, 0:W], r[:, R_E, 0:W], ACT.Exp).then_inc(ee_ready, 1)
                act.wait_ge(oddsc_ready, a + 1)
                act.activation(r[:, R_S, 0:W], r[:, R_S, 0:W], ACT.Ln, bias=one[:, :], scale=1.0).then_inc(s_ready, 1)
                act.wait_ge(c_ready, a + 1)
                act.activation(r[:, R_P, 0:W], r[:, R_C, 0:W], ACT.Exp, scale=p_sign[:, :]).then_inc(p_ready, 1)
                act.wait_ge(qk_ready, a + 1)
                dst = k_c[:, :] if W == CLS else r[0:M, R_K, 0:W]
                act.dma_start(dst, r[M:P, R_QK, 0:W]).then_inc(k_in, 16)

            def attn3(a):
                W, TP, nt = width(a)
                act.wait_ge(at_psum, a + 1)
                if nt == 1:
                    act.activation(v_c[:, :], v[0:CLS, 0, :], ACT.Copy).then_inc(at_rest, 1)
                    return
                act.wait_ge(at_diag, a + 1)
                for j in range(nt - 1):
                    act.activation(at[:, j, P:W - P * j], ps[:, PB0 + j, P:W - P * j], ACT.Copy)
                act.activation(r[0:1, R_C, 0:W], ps[0:1, DN0, 0:W], ACT.Copy).then_inc(at_rest, 1)

            def attn6(a):
                W, TP, nt = width(a)
                act.wait_ge(xpose2, a + 1)
                act.activation(xt_a[:, 0:W], ps[:, DN0, 0:W], ACT.Identity, bias=gb_a[:, 1:2],
                               scale=gb_a[:, 0:1]).then_inc(nta_ready, 1)

            def attn8(a):
                W, TP, nt = width(a)
                _, _, _, xh_a_, _, xh_b_, _, _ = tiles(a)
                act.wait_ge(xpose3, a + 1)
                act.activation(xh_a_[:, 0:W], ps[:, PB0 + 2, 0:W], ACT.Copy)
                act.activation(xh_b_[:, 0:W], ps[:, PB0 + 3, 0:W], ACT.Copy).then_inc(xh_ready, 1)

            def router(a):
                W, TP, nt = width(a)
                act.wait_ge(dz_ready, a + 1)
                act.activation(ez[0:TP, 0:nt, :], dz[0:TP, 0:nt, :], ACT.Exp).then_inc(ez_ready, 1)

            def gates(a):
                W, TP, nt = width(a)
                gate_ = tiles(a)[-1]
                act.wait_ge(gt_psum, a + 1)
                act.activation(gate_[:, 0:W], ps[0:GR, DN0 + 1, 0:W], ACT.Copy).then_inc(gate_ready, 1)

            def silu(f, c, cls=False):
                q = NC * f + c
                act.wait_ge(m_psum if cls else g_psum, q + 1)
                if c >= 2:
                    act.wait_ge(t_ready, q - 1)
                if cls:
                    dst, src = act_c[:, c % 2, :], ps[:, TB0, 0:CLS]
                else:
                    dst, src = r[:, c % 2, :], ps[:, PB0 + 2 * (c % 2), :]
                act.activation(dst, src, ACT.Silu).then_inc(silu_ready, 1)

            def split_hi_piece(p):
                act.wait_ge(wgu_raw, 48 * (p + 1))
                cut = slice(PC * p, PC * (p + 1))
                act.activation(wa_hi[:, cut, :, :].rearrange("p c t n -> p (c t n)"),
                               h2[:, :, :].rearrange("p a b -> p (a b)"), ACT.Copy).then_inc(split_hi, 1)
                act.activation(wb[:, cut, :, :].rearrange("p c t n -> p (c t n)"),
                               xn[:, :, :].rearrange("p a b -> p (a b)")[:, 0:PC * 2 * P], ACT.Copy).then_inc(split_hi, 1)

            act.wait_ge(consts_ok, 1)
            sines(0, 0)
            sines(0, 1)
            attn1(0)
            sines(0, 2)
            act.wait_ge(consts_ok, 2)
            attn2(0)
            attn3(0)
            attn6(0)
            attn8(0)
            router(0)
            gates(0)
            for k in range(3, NG):
                sines(0, k)
                split_hi_piece(k - 3)
            take_h(0)

            def body(a):
                sines(a, 0)
                sines(a, 1)
                attn1(a)
                sines(a, 2)
                attn2(a)
                sines(a, 3)
                attn3(a)
                sines(a, 4)
                sines(a, 5)
                attn6(a)
                sines(a, 6)
                sines(a, 7)
                attn8(a)
                sines(a, 8)
                router(a)
                gates(a)
                take_h(a)
                for c in range(NC):
                    silu(a - 1, c)

            for a in range(1, B):
                body(a)

            steps = [lambda: attn1(B), lambda: attn2(B), lambda: attn3(B), None, lambda: attn6(B), None,
                     lambda: attn8(B), lambda: router(B), lambda: gates(B)]
            for n, step in enumerate(steps):
                if step:
                    step()
                silu(B - 1, 2 * n, cls=True)
                silu(B - 1, 2 * n + 1, cls=True)
            for c in range(NC):
                silu(B, c)

        @block.vector
        def _(dve):
            def layernorm(src, dst, a, which, TP, nt, done, twice=False):
                n0 = (3 * a + which) * LNS
                step = [0]

                def next_(ins):
                    step[0] += 1
                    ins.then_inc(ln_step, 1)
                    dve.wait_ge(ln_step, n0 + step[0])

                for i in range(nt):
                    ins = dve.bn_stats(st[0:TP, i, :], src[0:TP, i, 0:D])
                next_(ins)
                for i in range(nt):
                    ins = dve.bn_aggr(mv[0:TP, i, :], st[0:TP, i, :])
                next_(ins)
                v_, y_, a_ = ve[0:TP, 0:nt], y[0:TP, 0:nt], ya[0:TP, 0:nt]
                next_(dve.tensor_scalar(v_, mv[0:TP, 0:nt, 1], LN_EPS, None, ALU.add))
                next_(dve.tensor_scalar(y_.bitcast(I32), v_.bitcast(I32), 1, None, ALU.logical_shift_right))
                next_(dve.tensor_scalar(y_.bitcast(I32), y_.bitcast(I32), -1.0, RSQRT_SEED, ALU.mult, ALU.add))
                for _ in range(3):
                    next_(dve.scalar_tensor_tensor(a_, y_, -0.5, y_, ALU.mult, ALU.mult))
                    next_(dve.tensor_tensor(a_, a_, v_, ALU.mult))
                    next_(dve.scalar_tensor_tensor(y_, a_, 1.5, y_, ALU.add, ALU.mult))
                for i in range(nt):
                    ins = dve.tensor_scalar(dst[0:TP, i, 0:D], src[0:TP, i, 0:D], mv[0:TP, i, 0:1], y[0:TP, i:i + 1],
                                            ALU.subtract, ALU.mult)
                    if twice:
                        ins = dve.tensor_scalar(dst[0:TP, i, D:D + DB], src[0:TP, i, P:D], mv[0:TP, i, 0:1],
                                                y[0:TP, i:i + 1], ALU.subtract, ALU.mult)
                ins.then_inc(done, 1)

            def remainders(a, k):
                q = NG * a + k
                s = k % SLOTS
                dve.wait_ge(n_ready, q + 1)
                for i in range(3):
                    fi = f_index(k, i)
                    ins = dve.scalar_tensor_tensor(feat[:, s, i, :], x[:, x_block(k), :], f_col[:, fi:fi + 1],
                                                   feat[:, s, i, :], ALU.mult, ALU.subtract)
                ins.then_inc(r_raw, 1)
                dve.wait_ge(r_raw, q + 1)
                dve.tensor_scalar(feat[:, s, 3:6, :].bitcast(I32), feat[:, s, 0:3, :].bitcast(I32), 0x7FFFFFFF, None,
                                  ALU.bitwise_and).then_inc(r_ready, 1)

            def attn0(a):
                W, TP, nt = width(a)
                h_, _, xn_ = tiles(a)[:3]
                if isinstance(a, int) and a == 0:
                    dve.wait_ge(cls_in, 16)
                else:
                    dve.wait_ge(h_ready, a)
                    dve.wait_ge(xpose3, a)
                layernorm(h_, xn_, a, 0, TP, nt, xn_ready)

            def attn1(a):
                W, TP, nt = width(a)
                dve.wait_ge(xpose1, a + 1)
                if not (isinstance(a, int) and a < 2):
                    dve.wait_ge(out_ready, a - 1)
                    dve.wait_ge(down_ready, NC * (a - 1))
                dve.tensor_copy(xt_b[:, 0:W], ps[0:DB, PB0 + 1, 0:W]).then_inc(xtb_ready, 1)

            def attn2(a):
                W, TP, nt = width(a)
                dve.wait_ge(qk_psum, a + 1)
                dve.tensor_scalar(r[:, R_E, 0:W], ps[:, PB0 + 2, 0:W], 0.0, None, ALU.min).then_inc(e_ready, 1)
                dve.wait_ge(odds_ready, a + 1)
                dve.tensor_scalar(r[:, R_S, 0:W], r[:, R_S, 0:W], MAX_ODDS, None, ALU.min).then_inc(oddsc_ready, 1)
                dve.wait_ge(ee_ready, a + 1)
                dve.scalar_tensor_tensor(r[:, R_PHI, 0:W], ps[:, PB0 + 2, 0:W], 0.0, r[:, R_E, 0:W],
                                         ALU.max, ALU.add).then_inc(phi_ready, 1)
                dve.wait_ge(s_ready, a + 1)
                first = isinstance(a, int) and a == 0
                dve.tensor_tensor_scan(r[:, R_C, 0:W], one[:, 0:1].to_broadcast([P, W]), r[:, R_S, 0:W],
                                       0.0 if first else s_c[:, 0:1], ALU.mult, ALU.add).then_inc(scan_ready, 1)
                dve.wait_ge(scan_ready, a + 1)
                if first:
                    dve.tensor_copy(s_c[:, :], r[:, R_S, 0:1])
                dve.tensor_scalar(r[:, R_C, 0:W], r[:, R_C, 0:W], CLIP, -CLIP, ALU.min, ALU.max).then_inc(c_ready, 1)
                dve.wait_ge(p_ready, a + 1)
                dve.wait_ge(phi_ready, a + 1)
                dve.scalar_tensor_tensor(r[:, R_QK, 0:W], r[:, R_PHI, 0:W], qk_scale[:, 0:1], r[:, R_P, 0:W],
                                         ALU.mult, ALU.mult).then_inc(qk_ready, 1)

            def attn3(a):
                W, TP, nt = width(a)
                dve.wait_ge(at_psum, a + 1)
                for j in range(nt):
                    ins = dve.tensor_tensor(at[0:TP, j, 0:TP], ps[0:TP, PB0 + j, 0:TP], causal[0:TP, 0:TP], ALU.mult)
                ins.then_inc(at_diag, 1)

            def attn5(a):
                W, TP, nt = width(a)
                xn_ = tiles(a)[2]
                dve.wait_ge(av_psum, a + 1)
                dve.tensor_scalar(den[0:TP, 0:nt], ps[0:TP, PB0:PB0 + nt, D], DEN_EPS, None,
                                  ALU.add).then_inc(den_ready, 1)
                dve.wait_ge(den_ready, a + 1)
                dve.reciprocal(rden[0:TP, 0:nt], den[0:TP, 0:nt]).then_inc(rden_ready, 1)
                dve.wait_ge(rden_ready, a + 1)
                for i in range(nt):
                    ins = dve.tensor_scalar(xn_[0:TP, i, 0:D], ps[0:TP, PB0 + i, 0:D], rden[0:TP, i:i + 1], None,
                                            ALU.mult)
                ins.then_inc(hh_ready, 1)
                dve.wait_ge(hh_ready, a + 1)
                layernorm(xn_, xn_, a, 1, TP, nt, hn_ready)

            def attn6(a):
                W, TP, nt = width(a)
                dve.wait_ge(xpose2, a + 1)
                dve.tensor_scalar(xt_b[:, 0:W], ps[0:DB, DN0 + 1, 0:W], gb_b[:, 0:1], gb_b[:, 1:2], ALU.mult,
                                  ALU.add).then_inc(ntb_ready, 1)

            def attn7(a):
                W, TP, nt = width(a)
                h_, h2_, xn_ = tiles(a)[:3]
                dve.wait_ge(wo_psum, a + 1)
                if not (isinstance(a, int) and a < 2):
                    dve.wait_ge(out_dma, 16 * (a - 1))
                n = min(2, nt)
                for i in range((nt + 1) // 2):
                    ins = dve.tensor_tensor(
                        h2_[0:TP, 2 * i:2 * i + n, :], h_[0:TP, 2 * i:2 * i + n, :],
                        ps[0:TP, PB0 + i, 0:n * D].rearrange("p (t d) -> p t d", d=D), ALU.add)
                ins.then_inc(h2_ready, 1)
                dve.wait_ge(h2_ready, a + 1)
                layernorm(h2_, xn_, a, 2, TP, nt, xn2_ready, twice=True)

            def attn8(a):
                W, TP, nt = width(a)
                _, _, _, xh_a_, xl_a_, xh_b_, xl_b_, _ = tiles(a)
                dve.wait_ge(xh_ready, a + 1)
                dve.tensor_tensor(xl_a_[:, 0:W], ps[:, PB0 + 2, 0:W], xh_a_[:, 0:W].bitcast(F32), ALU.subtract)
                dve.tensor_tensor(xl_b_[:, 0:W], ps[0:DB, PB0 + 3, 0:W], xh_b_[0:DB, 0:W].bitcast(F32),
                                  ALU.subtract).then_inc(xl_ready, 1)

            TOPS = 12

            def router(a):
                W, TP, nt = width(a)
                step = [0]

                def next_(ins):
                    step[0] += 1
                    ins.then_inc(top_step, 1)
                    dve.wait_ge(top_step, TOPS * a + step[0])

                L, L2, K = lg[0:TP, 0:nt, 0:NE], lg2[0:TP, 0:nt, :], key[0:TP, 0:nt, :]
                ranks = rank[0:TP, :].unsqueeze(1).to_broadcast([TP, nt, NE])

                def wide(t):
                    return t.unsqueeze(2).to_broadcast([TP, nt, NE])

                dve.wait_ge(lg_psum, a + 1)
                next_(dve.tensor_copy(lg[0:TP, 0:nt, :], ps[0:TP, DN0, 0:16 * nt].rearrange(
                    "p (t n) -> p t n", n=16)[:, :, 0:NE + 1]))
                for row, (src, oh) in enumerate(((L, oh1[0:TP, 0:nt, :]), (L2, oh2[0:TP, 0:nt, :]))):
                    best, at_ = top[0:TP, 2 * row, 0:nt], top[0:TP, 2 * row + 1, 0:nt]
                    next_(dve.tensor_reduce(best, src, AX_X, ALU.max))
                    next_(dve.tensor_tensor(K, src, wide(best), ALU.is_equal))
                    next_(dve.tensor_tensor(K, K, ranks, ALU.mult))
                    next_(dve.tensor_reduce(at_, K, AX_X, ALU.max))
                    next_(dve.tensor_tensor(oh, K, wide(at_), ALU.is_equal))
                    if row == 0:
                        next_(dve.scalar_tensor_tensor(L2, oh, -FAR, L, ALU.mult, ALU.add))
                assert step[0] == TOPS
                dve.tensor_tensor(dz[0:TP, 0:nt, 0], top[0:TP, 2, 0:nt], top[0:TP, 0, 0:nt], ALU.subtract)
                dve.tensor_scalar(dz[0:TP, 0:nt, 1], lg[0:TP, 0:nt, NE], sgb[0:TP, 0:1], -1.0, ALU.add,
                                  ALU.mult).then_inc(dz_ready, 1)
                dve.wait_ge(ez_ready, a + 1)
                gstep = [0]

                def gnext(ins):
                    gstep[0] += 1
                    ins.then_inc(gt_step, 1)
                    dve.wait_ge(gt_step, 8 * a + gstep[0])

                e, iz_ = ez[0:TP, 0:nt, :], iz[0:TP, 0:nt, :]
                gnext(dve.tensor_scalar(iz_, e, 1.0, None, ALU.add))
                gnext(dve.reciprocal(iz_, iz_))
                dve.tensor_tensor(ga[0:TP, 0:nt, 1], e[:, :, 0], iz_[:, :, 0], ALU.mult)
                gnext(dve.tensor_scalar(ga[0:TP, 0:nt, 2], iz_[:, :, 1], -1.0, 1.0, ALU.mult, ALU.add))
                dve.tensor_tensor(ga[0:TP, 0:nt, 0], iz_[:, :, 0], ga[0:TP, 0:nt, 2], ALU.mult)
                gnext(dve.tensor_tensor(ga[0:TP, 0:nt, 1], ga[0:TP, 0:nt, 1], ga[0:TP, 0:nt, 2], ALU.mult))
                dve.tensor_tensor(oh1[0:TP, 0:nt, :], oh1[0:TP, 0:nt, :], wide(ga[0:TP, 0:nt, 0]), ALU.mult)
                gnext(dve.tensor_tensor(oh2[0:TP, 0:nt, :], oh2[0:TP, 0:nt, :], wide(ga[0:TP, 0:nt, 1]), ALU.mult))
                dve.tensor_tensor(gm[0:TP, 0:nt, 0:NE], oh1[0:TP, 0:nt, :], oh2[0:TP, 0:nt, :], ALU.add)
                gnext(dve.tensor_copy(gm[0:TP, 0:nt, NE], iz_[:, :, 1]))
                gnext(dve.tensor_copy(gm_hi[0:TP, 0:nt, :], gm[0:TP, 0:nt, :]))
                dve.tensor_copy(gt[0:TP, 0:nt, 0:NE + 1], gm_hi[0:TP, 0:nt, :].bitcast(F32))
                gnext(dve.tensor_tensor(gt[0:TP, 0:nt, GLO:GR], gm[0:TP, 0:nt, :], gm_hi[0:TP, 0:nt, :].bitcast(F32),
                                        ALU.subtract))
                assert gstep[0] == 8

            def hidden(f, c, cls=False):
                q = NC * f + c
                s = c % 2
                if cls:
                    S_, t_, hid_ = act_c[:, s, :], act_c[:, 2 + s, :], act_c[:, 4 + c % 3, :]
                    u_, m_ = ps[:, TB0, CLS:2 * CLS], ps[:, TB0, 2 * CLS:3 * CLS]
                else:
                    S_, t_, hid_ = r[:, s, :], r[:, 2 + s, :], r[:, 4 + c % 3, :]
                    u_, m_ = ps[:, PB0 + 2 * s + 1, :], ps[:, TB0 + s, :]
                dve.wait_ge(u_psum, q + 1)
                dve.wait_ge(silu_ready, q + 1)
                if c >= 2:
                    dve.wait_ge(hid_ready, q - 1)
                dve.tensor_tensor(t_, S_, u_, ALU.mult).then_inc(t_ready, 1)
                dve.wait_ge(t_ready, q + 1)
                dve.wait_ge(m_psum, q + 1)
                if c >= 3:
                    dve.wait_ge(down_ready, q - 2)
                dve.tensor_tensor(hid_, t_, m_, ALU.mult).then_inc(hid_ready, 1)

            def finish(f, cls=False):
                dve.wait_ge(down_ready, NC * (f + 1))
                if cls:
                    dve.tensor_tensor(h2_c[:, 0, :], h2_c[:, 0, :], ps[0:CLS, TB0 + 1, 0:D],
                                      ALU.add).then_inc(out_ready, 1)
                    return
                for i in range(2):
                    ins = dve.tensor_tensor(
                        h2[:, 2 * i:2 * i + 2, :], h2[:, 2 * i:2 * i + 2, :],
                        ps[:, DN0 + i, 0:2 * D].rearrange("p (t d) -> p t d", d=D), ALU.add)
                ins.then_inc(out_ready, 1)

            def split_piece(p):
                cut = slice(PC * p, PC * (p + 1))
                dve.wait_ge(split_hi, 2 * p + 2)
                dve.tensor_tensor(wa_lo[:, cut, :, :].rearrange("p c t n -> p (c t n)"),
                                  h2[:, :, :].rearrange("p a b -> p (a b)"),
                                  wa_hi[:, cut, :, :].rearrange("p c t n -> p (c t n)").bitcast(F32),
                                  ALU.subtract).then_inc(split_done, 1)
                low = wb[DB:P, cut, :, :].rearrange("p c t n -> p (c t n)")
                dve.tensor_tensor(low, xn[DB:P, :, :].rearrange("p a b -> p (a b)")[:, 0:PC * 2 * P], low.bitcast(F32),
                                  ALU.subtract).then_inc(split_done, 1)

            dve.memset(half_pi[:, :], HALF_PI)
            dve.memset(wr_raw[:, :, :], 0.0).then_inc(consts_ok, 1)
            dve.memset(one[:, :], 1.0)
            dve.memset(v[:, :, D:D + 1], 1.0)
            dve.memset(gt[:, :, :], 0.0)
            dve.memset(qk_scale[0:M, :], float(M) ** -0.5)
            dve.memset(qk_scale[M:P, :], 1.0)
            dve.memset(p_sign[0:M, :], -1.0)
            dve.memset(p_sign[M:P, :], 1.0)
            dve.wait_ge(w_small, 16 * N_SMALL)
            dve.tensor_scalar(neg_bf[:, :], neg_bf[:, :], -1.0, None, ALU.mult)
            dve.tensor_copy(pick[:, :, :], pick_raw[:, :].unsqueeze(2).to_broadcast([GR, NE + 1, P // 2])).then_inc(consts_ok, 1)
            remainders(0, 0)
            remainders(0, 1)
            dve.wait_ge(router_hi, 16 * 6)
            dve.tensor_copy(wra_hi[:, :], wr_raw[:, 0, :])
            dve.tensor_copy(wrb[:, :], wr_raw[:, 1, :]).then_inc(router_split, 1)
            dve.wait_ge(router_split, 1)
            dve.tensor_tensor(wra_lo[:, :], wr_raw[:, 0, :], wra_hi[:, :].bitcast(F32), ALU.subtract)
            dve.tensor_tensor(wrb[DB:P, :], wr_raw[DB:P, 1, :], wrb[DB:P, :].bitcast(F32),
                              ALU.subtract).then_inc(router_split, 1)
            attn0(0)
            attn1(0)
            remainders(0, 2)
            attn2(0)
            attn3(0)
            attn5(0)
            attn6(0)
            attn7(0)
            attn8(0)
            router(0)
            for k in range(3, NG):
                remainders(0, k)
                split_piece(k - 3)
            dve.wait_ge(split_done, 2 * PIECES)
            attn0(1)

            def body(a):
                remainders(a, 0)
                remainders(a, 1)
                attn1(a)
                remainders(a, 2)
                attn2(a)
                remainders(a, 3)
                attn3(a)
                remainders(a, 4)
                attn5(a)
                remainders(a, 5)
                attn6(a)
                remainders(a, 6)
                attn7(a)
                remainders(a, 7)
                attn8(a)
                remainders(a, 8)
                router(a)
                attn0(a + 1)
                for c in range(NC):
                    hidden(a - 1, c)
                finish(a - 1)

            for a in range(1, B):
                body(a)

            steps = [attn1, attn2, attn3, attn5, attn6, attn7, attn8, router, None]
            for n, step in enumerate(steps):
                if step:
                    step(B)
                hidden(B - 1, 2 * n, cls=True)
                hidden(B - 1, 2 * n + 1, cls=True)
            finish(B - 1, cls=True)
            for c in range(NC):
                hidden(B, c)
            finish(B)

        @block.tensor
        def _(pe):
            def project(a, k):
                q = NG * a + k
                if isinstance(a, int) and a == 0:
                    pe.wait_ge(wt_in[k], x_parts(k))
                elif k == 0:
                    pe.wait_ge(h_ready, a)
                if k == 0 and not (isinstance(a, int) and a < 2):
                    pe.wait_ge(hid_ready, NC * (a - 1))
                pe.wait_ge(sin_ready, q + 1)
                for i in range(6):
                    for t in range(NT):
                        ins = pe.matmul(ps[:, TB0 + t // 2, (t % 2) * D:(t % 2 + 1) * D],
                                        feat[:, k % SLOTS, i, t * P:(t + 1) * P], w_tok[:, k, i, :],
                                        start=(k == 0 and i == 0 and t % 2 == 0), stop=(k == NG - 1 and i == 5),
                                        skip_group_check=True)
                ins.then_inc(tok_group, 1)

            def attn1(a):
                W, TP, nt = width(a)
                xn_ = tiles(a)[2]
                pe.wait_ge(xn_ready, a + 1)
                if not (isinstance(a, int) and a < 2):
                    pe.wait_ge(silu_ready, NC * (a - 1))
                    pe.wait_ge(t_ready, NC * (a - 1))
                for i in range(nt):
                    pe.transpose(ps[:, PB0, i * P:i * P + TP], xn_[0:TP, i, 0:P], ident[0:TP, 0:TP])
                for i in range(nt):
                    ins = pe.transpose(ps[0:DB, PB0 + 1, i * P:i * P + TP], xn_[0:TP, i, P:D], ident[0:TP, 0:TP])
                ins.then_inc(xpose1, 1)

            def attn2(a):
                W, TP, nt = width(a)
                pe.wait_ge(xta_ready, a + 1)
                pe.wait_ge(xtb_ready, a + 1)

                def pair(bank, wa, wb_):
                    pe.matmul(ps[:, bank, 0:W], wa.rearrange("k a b -> k (a b)"), xt_a[:, 0:W], start=True, stop=False)
                    return pe.matmul(ps[:, bank, 0:W], wb_.rearrange("k a b -> k (a b)"), xt_b[:, 0:W],
                                     start=False, stop=True)

                pair(PB0 + 3, wff_a[:, :, :], wff_b[:, :, :]).then_inc(f_psum, 1)
                pair(PB0 + 2, wqk_a[:, :, :], wqk_b[:, :, :]).then_inc(qk_psum, 1)
                if not (isinstance(a, int) and a == 0):
                    pe.wait_ge(gate_ready, a)
                if not (isinstance(a, int) and a < 2):
                    pe.wait_ge(out_ready, a - 1)
                for i in range(nt):
                    o = ps[0:TP, DN0 + i // 2, (i % 2) * D:(i % 2 + 1) * D]
                    pe.matmul(o, xt_a[:, i * P:i * P + TP], wv_a[:, :], start=True, stop=False)
                    ins = pe.matmul(o, xt_b[:, i * P:i * P + TP], wv_b[:, :], start=False, stop=True)
                ins.then_inc(v_psum, 1)

            def attn3(a):
                W, TP, nt = width(a)
                pe.wait_ge(k_in, 16 * (a + 1))
                pe.wait_ge(qk_ready, a + 1)
                pe.wait_ge(v_ready, a + 1)
                k_ = k_c[:, :] if nt == 1 else r[0:M, R_K, :]
                if nt > 1:
                    pe.matmul(ps[0:1, DN0, 0:W], k_c[:, 0:1], r[0:M, R_QK, 0:W], start=True, stop=True)
                for j in range(nt):
                    ins = pe.matmul(ps[0:TP, PB0 + j, 0:W - P * j], k_[:, j * P:j * P + TP],
                                    r[0:M, R_QK, j * P:W], start=True, stop=True)
                ins.then_inc(at_psum, 1)

            def attn5(a):
                W, TP, nt = width(a)
                pe.wait_ge(at_diag, a + 1)
                pe.wait_ge(at_rest, a + 1)
                for i in range(nt):
                    o = ps[0:TP, PB0 + i, 0:D + 1]
                    if nt > 1:
                        pe.matmul(o, r[0:1, R_C, i * P:(i + 1) * P], v_c[0:1, :], start=True, stop=False)
                    for j in range(i + 1):
                        ins = pe.matmul(o, at[0:TP, j, (i - j) * P:(i - j) * P + TP], v[0:TP, j, :],
                                        start=(nt == 1), stop=(j == i))
                ins.then_inc(av_psum, 1)

            def attn6(a):
                W, TP, nt = width(a)
                xn_ = tiles(a)[2]
                pe.wait_ge(hn_ready, a + 1)
                for i in range(nt):
                    pe.transpose(ps[:, DN0, i * P:i * P + TP], xn_[0:TP, i, 0:P], ident[0:TP, 0:TP])
                for i in range(nt):
                    ins = pe.transpose(ps[0:DB, DN0 + 1, i * P:i * P + TP], xn_[0:TP, i, P:D], ident[0:TP, 0:TP])
                ins.then_inc(xpose2, 1)

            def attn7(a):
                W, TP, nt = width(a)
                pe.wait_ge(nta_ready, a + 1)
                pe.wait_ge(ntb_ready, a + 1)
                for i in range(nt):
                    o = ps[0:TP, PB0 + i // 2, (i % 2) * D:(i % 2 + 1) * D]
                    pe.matmul(o, xt_a[:, i * P:i * P + TP], wo_a[:, :], start=True, stop=False)
                    ins = pe.matmul(o, xt_b[:, i * P:i * P + TP], wo_b[:, :], start=False, stop=True)
                ins.then_inc(wo_psum, 1)

            def attn8(a):
                W, TP, nt = width(a)
                xn_ = tiles(a)[2]
                pe.wait_ge(xn2_ready, a + 1)
                for i in range(nt):
                    pe.transpose(ps[:, PB0 + 2, i * P:i * P + TP], xn_[0:TP, i, 0:P], ident[0:TP, 0:TP])
                for i in range(nt):
                    ins = pe.transpose(ps[:, PB0 + 3, i * P:i * P + TP], xn_[0:TP, i, P:D + DB], ident[0:TP, 0:TP])
                ins.then_inc(xpose3, 1)

            def router(a):
                W, TP, nt = width(a)
                _, _, _, xh_a_, xl_a_, xh_b_, xl_b_, _ = tiles(a)
                pe.wait_ge(xh_ready, a + 1)
                pe.wait_ge(xl_ready, a + 1)
                for i in range(nt):
                    o, c = ps[0:TP, DN0, 16 * i:16 * i + NR], slice(i * P, i * P + TP)
                    pe.matmul(o, xh_a_[:, c], wra_hi[:, :], start=True, stop=False)
                    pe.matmul(o, xh_a_[:, c], wra_lo[:, :], start=False, stop=False)
                    pe.matmul(o, xl_a_[:, c], wra_hi[:, :], start=False, stop=False)
                    pe.matmul(o, xh_b_[:, c], wrb[:, :], start=False, stop=False)
                    ins = pe.matmul(o, xl_b_[:, c], wrb[0:DB, :], start=False, stop=True)
                ins.then_inc(lg_psum, 1)

            def gates(a):
                W, TP, nt = width(a)
                pe.wait_ge(gt_step, 8 * (a + 1))
                for i in range(nt):
                    ins = pe.transpose(ps[0:GR, DN0 + 1, i * P:i * P + TP], gt[0:TP, i, :], ident[0:TP, 0:TP])
                ins.then_inc(gt_psum, 1)

            def up(f, c, cls=False):
                q = NC * f + c
                if cls:
                    xh, xl, yh, yl, gate_ = xhc_a, xlc_a, xhc_b, xlc_b, gatec_t
                    outs = [ps[:, TB0, CLS * i:CLS * (i + 1)] for i in range(3)]
                    if c >= 1:
                        pe.wait_ge(silu_ready, q)
                        pe.wait_ge(hid_ready, q)
                else:
                    xh, xl, yh, yl, gate_ = xh_a, xl_a, xh_b, xl_b, gate_t
                    outs = [ps[:, PB0 + 2 * (c % 2) + i, :] for i in range(2)] + [ps[:, TB0 + c % 2, :]]
                    if c >= 2:
                        pe.wait_ge(silu_ready, q - 1)
                        pe.wait_ge(t_ready, q - 1)
                for i, done in enumerate((g_psum, u_psum)):
                    o = outs[i]
                    pe.matmul(o, wa_hi[:, c, i, :], xh[:, :], start=True, stop=False)
                    pe.matmul(o, wa_lo[:, c, i, :], xh[:, :], start=False, stop=False)
                    pe.matmul(o, wa_hi[:, c, i, :], xl[:, :], start=False, stop=False)
                    pe.matmul(o, wb[:, c, i, :], yh[:, :], start=False, stop=False)
                    pe.matmul(o, wb[0:DB, c, i, :], yl[:, :], start=False, stop=True).then_inc(done, 1)
                if not cls and c >= 2:
                    pe.wait_ge(hid_ready, q - 1)
                e0 = NE if c < NCS else (c - NCS) * P // D
                e1 = NE if c < NCS else ((c - NCS) * P + P - 1) // D
                sel = (pick[:, e0, 0:1].to_broadcast([GR, P]) if e0 == e1 else
                       pick[:, e0:e0 + 2, :].rearrange("k e m -> k (e m)"))
                pe.matmul(outs[2], sel, gate_[:, :], start=True, stop=True).then_inc(m_psum, 1)

            def down(f, c, cls=False):
                q = NC * f + c
                pe.wait_ge(hid_ready, q + 1)
                for t in range(1 if cls else NT):
                    if cls:
                        o, hid = ps[0:CLS, TB0 + 1, 0:D], act_c[:, 4 + c % 3, :]
                    else:
                        o, hid = ps[:, DN0 + t // 2, (t % 2) * D:(t % 2 + 1) * D], r[:, 4 + c % 3, t * P:(t + 1) * P]
                    ins = pe.matmul(o, hid, w_down[:, c, :], start=(c == 0 and t % 2 == 0), stop=(c == NC - 1),
                                    skip_group_check=True)
                ins.then_inc(down_ready, 1)

            def ffn_step(f, c, cls=False):
                if c < NC:
                    up(f, c, cls)
                if c >= 2:
                    down(f, c - 2, cls)

            pe.wait_ge(w_small, 16 * N_SMALL)
            attn1(0)
            project(0, 0)
            pe.wait_ge(consts_ok, 2)
            attn2(0)
            project(0, 1)
            attn3(0)
            attn5(0)
            attn6(0)
            project(0, 2)
            attn7(0)
            attn8(0)
            pe.wait_ge(router_split, 2)
            router(0)
            gates(0)
            for k in range(3, NG):
                project(0, k)

            pe.wait_ge(split_done, 2 * PIECES)
            pe.wait_ge(wdown_in, 16)

            def body(a):
                attn1(a)
                project(a, 0)
                attn2(a)
                project(a, 1)
                project(a, 2)
                attn3(a)
                project(a, 3)
                attn5(a)
                project(a, 4)
                attn6(a)
                project(a, 5)
                attn7(a)
                project(a, 6)
                attn8(a)
                project(a, 7)
                router(a)
                project(a, 8)
                gates(a)
                pe.wait_ge(h_ready, a + 1)
                pe.wait_ge(gate_ready, a + 1)
                for c in range(NC + 2):
                    ffn_step(a - 1, c)

            for a in range(1, B):
                body(a)

            steps = [attn1, attn2, attn3, attn5, attn6, attn7, attn8, router, gates]
            pe.wait_ge(hid_ready, NC * (B - 1))
            for n, step in enumerate(steps):
                step(B)
                ffn_step(B - 1, 2 * n, cls=True)
                ffn_step(B - 1, 2 * n + 1, cls=True)
            ffn_step(B - 1, NC, cls=True)
            ffn_step(B - 1, NC + 1, cls=True)
            pe.wait_ge(out_ready, B)
            pe.wait_ge(gate_ready, B + 1)
            for c in range(NC + 2):
                ffn_step(B, c)


def kernel(x, cls_tok, L0_tok_freq_bands, L0_tok_W, L0_attn_Wq, L0_attn_Wk, L0_attn_Wv, L0_attn_Wf, L0_attn_bf,
           L0_attn_Wo, L0_attn_gamma, L0_attn_beta, L0_ffn_router_w, L0_ffn_w_gate, L0_ffn_w_up, L0_ffn_w_down,
           L0_ffn_ws_gate, L0_ffn_ws_up, L0_ffn_ws_down, L0_ffn_sg_w, L0_ffn_sg_b):
    import concourse.bacc as bacc
    from concourse.bass_utils import run_bass_kernel_spmd

    def experts(w):
        return np.asarray(w).transpose(1, 0, 2).reshape(D, NE * D)

    gate = np.concatenate([np.asarray(L0_ffn_ws_gate), experts(L0_ffn_w_gate)], axis=1)
    up = np.concatenate([np.asarray(L0_ffn_ws_up), experts(L0_ffn_w_up)], axis=1)
    consts = np.zeros((P, 2 * P + 2 * NE + 1), np.float32)
    consts[:, 0:P] = np.eye(P, dtype=np.float32)
    consts[:, P:2 * P] = np.triu(np.ones((P, P), np.float32))
    for e in range(NE + 1):
        consts[e, 2 * P + e] = consts[GLO + e, 2 * P + e] = 1.0
    consts[:, 2 * P + NE + 1:] = np.arange(NE, 0, -1, dtype=np.float32)
    fr = np.asarray(L0_tok_freq_bands)
    arrays = {
        "xT": np.asarray(x).reshape(B, T, J).transpose(0, 2, 1),
        "wT": np.asarray(L0_tok_W).reshape(D, J, 2 * NF).transpose(1, 2, 0),
        "freqs": np.stack([np.concatenate([fr, fr[half::2]]) for half in range(2)]),
        "cls_tok": np.asarray(cls_tok).reshape(1, D),
        "wq": L0_attn_Wq, "wk": L0_attn_Wk, "wv": L0_attn_Wv, "wf": L0_attn_Wf,
        "bf": np.asarray(L0_attn_bf).reshape(M, 1),
        "gamma": np.asarray(L0_attn_gamma).reshape(D, 1),
        "beta": np.asarray(L0_attn_beta).reshape(D, 1),
        "wo": L0_attn_Wo, "wr": L0_ffn_router_w, "sg_w": L0_ffn_sg_w,
        "sg_b": np.asarray(L0_ffn_sg_b).reshape(1, 1),
        "wgu": np.stack([gate.reshape(D, NC, P), up.reshape(D, NC, P)], axis=2).reshape(D, NC, 2 * P),
        "wd": np.concatenate([np.asarray(L0_ffn_ws_down), np.asarray(L0_ffn_w_down).reshape(NE * D, D)], axis=0),
        "consts": consts,
    }
    arrays = {n: np.ascontiguousarray(a) for n, a in arrays.items()}
    nc = bacc.Bacc("TRN2", target_bir_lowering=False, num_devices=1)
    args = [nc.dram_tensor(f"in_{n}", a.shape, mybir.dt.from_np(a.dtype), kind="ExternalInput").ap()
            for n, a in arrays.items()]
    out = nc.dram_tensor("out", (B, T + 1, D), F32, kind="ExternalOutput").ap()
    build(nc, *args, out)
    res = run_bass_kernel_spmd(nc, [{f"in_{n}": a for n, a in arrays.items()}], core_ids=[0])
    return res.results[0]["out"]
```

```python
from contextlib import ExitStack

import numpy as np

import concourse.bass as bass
from concourse import mybir

F32 = mybir.dt.float32
F32R = mybir.dt.float32r
I32 = mybir.dt.int32
ALU = mybir.AluOpType
ACT = mybir.ActivationFunctionType
AX_X = mybir.AxisListType.X

P = 128
B = 4
C3 = 3
T = 512
D = 192
DB = D - P
NF = 6
M = 64
NE = 8
HS = 768
HID = HS + NE * D
NC = HID // P
NCS = HS // P
NT = T // P
J = C3 * D
JC = J // P
NG = 2 * JC + 1
SLOTS = 3
CLS = 2
NR = NE + 2
GLO = 32
GR = GLO + NE + 1
PIECES = 6
PC = NC // PIECES
LNS = 14
MAGIC = 1.5 * 2.0 ** 23
RSQRT_SEED = float(0x5F3759DF)
TWO_PI = float(np.float32(2.0 * np.pi))
HALF_PI = float(np.float32(0.5 * np.pi))
LN_EPS = 1e-5
DEN_EPS = 1e-6
MAX_ODDS = float(np.float32(1e6) - np.float32(1.0))
CLIP = 20.0
FAR = 1e30
TB0, G0, U0, M0, DN0, A0, A1, A2 = 0, 0, 1, 2, 3, 5, 6, 7
AT_X1, AT_QKV, AT_V23, AT_SCORES, AT_AV = 3, 5, 7, 13, 15
AT_X2, AT_WO, AT_X3, AT_LG, AT_GT = 1, 2, 4, 5, 7
CT_X2, CT_WO, CT_X3, CT_LG, CT_GT = 2, 5, 9, 12, 17
AT_AHEAD = (12, 14)
AV_BANK, WO_BANK = (A2, A1), (A1, A0)


def build(nc, xT, wT, freqs, cls_tok, wq, wk, wv, wf, bf, gamma, beta, wo,
          wr, sg_w, sg_b, wgu, wd, consts, out):
    with ExitStack() as ctx:
        def sb(name, shape, dt=F32):
            return ctx.enter_context(nc.sbuf_tensor(name, shape, dt))

        def sem(name):
            return ctx.enter_context(nc.semaphore(name))

        w_tok = sb("w_tok", [P, NG, 2 * 3, D])
        wa_hi = sb("wa_hi", [P, NC, 2, P], F32R)
        wa_lo = sb("wa_lo", [P, NC, 2, P], F32R)
        wb = sb("wb", [P, NC, 2, P], F32R)
        w_down = sb("w_down", [P, NC, D])
        wqk_a, wqk_b = sb("wqk_a", [P, 2, M]), sb("wqk_b", [P, 2, M])[DB:P]
        wff_a, wff_b = sb("wff_a", [P, 2, M]), sb("wff_b", [P, 2, M])[DB:P]
        wv_a, wv_b = sb("wv_a", [P, D]), sb("wv_b", [P, D])[DB:P]
        wo_a, wo_b = sb("wo_a", [P, D]), sb("wo_b", [P, D])[DB:P]
        gb_a, gb_b = sb("gb_a", [P, 2]), sb("gb_b", [DB, 2])
        neg_bf = sb("neg_bf", [P, 1])
        wr_raw = sb("wr_raw", [P, 2, NR])
        wra_hi, wra_lo, wrb = (sb(n, [P, NR], F32R) for n in ("wra_hi", "wra_lo", "wrb"))
        sgb = sb("sgb", [P, 1])
        f_col = sb("f_col", [P, NF + 3])
        ident, causal = sb("ident", [P, P]), sb("causal", [P, P])
        qk_scale, p_sign = sb("qk_scale", [P, 1]), sb("p_sign", [P, 1])
        half_pi = sb("half_pi", [P, 1])
        rank = sb("rank", [P, NE])
        pick_raw = sb("pick_raw", [GR, NE + 1])
        pick = sb("pick", [GR, NE + 1, P // 2], F32R)
        one = sb("one", [P, 1])
        x = sb("x", [P, JC + 1, T])
        feat = sb("feat", [P, SLOTS, 6, T])
        h, h2 = sb("h", [P, NT, D]), sb("h2", [P, NT, D])
        xn = sb("xn", [P, NT, D + DB])
        xt_a = sb("xt_a", [P, T])
        v = sb("v", [P, NT, D + 1])
        r = sb("r", [P, 7, T])
        xh_a, xl_a = sb("xh_a", [P, T], F32R), sb("xl_a", [P, T], F32R)
        xh_b, xl_b = sb("xh_b", [P, T], F32R), sb("xl_b", [DB, T], F32R)
        gate_t = sb("gate_t", [GR, T], F32R)
        h_c, xn_c = h[0:CLS, 0:1, :], xn[0:CLS, 0:1, :]
        h2_c = sb("h2_c", [CLS, 1, D])
        state = sb("state", [M, D + 1])
        s_c = sb("s_c", [P, 1])
        xhc_a, xlc_a = sb("xhc_a", [P, CLS], F32R), sb("xlc_a", [P, CLS], F32R)
        xhc_b, xlc_b = sb("xhc_b", [P, CLS], F32R), sb("xlc_b", [DB, CLS], F32R)
        gatec_t = sb("gatec_t", [GR, CLS], F32R)
        act_c = sb("act_c", [P, 7, CLS])
        st, mv = sb("st", [P, NT, 6]), sb("mv", [P, NT, 2])
        ve, y, ya = sb("ve", [P, NT]), sb("y", [P, NT]), sb("ya", [P, NT])
        den, rden = sb("den", [P, NT]), sb("rden", [P, NT])
        lg, lg2 = sb("lg", [P, NT, NE + 1]), sb("lg2", [P, NT, NE])
        top = sb("top", [P, 4, NT])
        oh1, oh2, key = sb("oh1", [P, NT, NE]), sb("oh2", [P, NT, NE]), sb("key", [P, NT, NE])
        dz, ez, iz = sb("dz", [P, NT, 2]), sb("ez", [P, NT, 2]), sb("iz", [P, NT, 2])
        ga = sb("ga", [P, NT, 3])
        gm = sb("gm", [P, NT, NE + 1])
        gm_hi = sb("gm_hi", [P, NT, NE + 1], F32R)
        gt = sb("gt", [P, NT, GR])

        ps = ctx.enter_context(nc.psum_tensor("ps", [P, 8, 512], F32))

        R_E, R_PHI, R_S, R_P, R_C, R_QK, R_K = range(7)
        at = r[:, 0:4, :]
        xt_b = r[DB:P, R_K, :]
        fr = feat[:, SLOTS - 1, :, :]
        F_S, F_T, F_H = 0, 2, 3

        names = """w_small f_in wgu_raw wdown_in cls_in split_hi split_done router_hi router_split consts_ok
            n_raw n_ready r_raw r_ready sin_ready tok_group
            h_ready ln_step xn_ready xpose1 xta_ready xtb_ready qk_psum f_psum v01_psum v23_psum v_ready
            e_ready ee_ready odds_ready oddsc_ready s_ready scan_ready c_ready p_ready phi_ready
            qk_ready k_in at_psum at_diag at_rest state_psum state_ready av_psum den_ready rden_ready hh_ready hn_ready
            xpose2 nta_ready ntb_ready wo_psum h2_ready xn2_ready xpose3 xh_ready xl_ready
            lg_psum top_step dz_ready ez_ready gt_step gt_psum gate_ready
            g_psum u_psum m_psum silu_ready t_ready hid_ready down_ready out_ready out_dma clsout_dma"""
        S = {n: sem(n) for n in names.split()}
        (w_small, f_in, wgu_raw, wdown_in, cls_in, split_hi, split_done, router_hi, router_split, consts_ok,
         n_raw, n_ready, r_raw, r_ready, sin_ready, tok_group,
         h_ready, ln_step, xn_ready, xpose1, xta_ready, xtb_ready, qk_psum, f_psum, v01_psum, v23_psum, v_ready,
         e_ready, ee_ready, odds_ready, oddsc_ready, s_ready, scan_ready, c_ready, p_ready, phi_ready,
         qk_ready, k_in, at_psum, at_diag, at_rest, state_psum, state_ready, av_psum, den_ready, rden_ready, hh_ready, hn_ready,
         xpose2, nta_ready, ntb_ready, wo_psum, h2_ready, xn2_ready, xpose3, xh_ready, xl_ready,
         lg_psum, top_step, dz_ready, ez_ready, gt_step, gt_psum, gate_ready,
         g_psum, u_psum, m_psum, silu_ready, t_ready, hid_ready, down_ready, out_ready, out_dma,
         clsout_dma) = (S[n] for n in names.split())
        wt_in = [sem(f"wt_in{k}") for k in range(NG)]
        xc_in = [sem(f"xc_in{k}") for k in range(JC + 1)]
        N_SMALL = 23

        def width(a):
            cls = a == 0
            return (CLS, CLS, 1) if cls else (T, P, NT)

        def tiles(a):
            if a == 0:
                return h_c, h2_c, xn_c, xhc_a, xlc_a, xhc_b, xlc_b, gatec_t
            return h, h2, xn, xh_a, xl_a, xh_b, xl_b, gate_t

        def score_place(j):
            return ((A2, 0), (A1, 0), (A0, 0), (A0, 2 * P))[j]

        def x_block(k):
            return k // 2 if k < 2 * JC else JC

        def x_parts(k):
            return 16 if k < 2 * JC else 32

        def f_index(k, i):
            return 3 * (k % 2) + i if k < 2 * JC else NF + i

        block = ctx.enter_context(nc.Block())

        @block.sync
        def _(sp):
            def small(dst, src):
                sp.dma_start(dst, src).then_inc(w_small, 16)

            def load_x(b, k):
                sem_ = xc_in[k]
                if k < JC:
                    sp.dma_start(x[:, k, :], xT[b, k * P:(k + 1) * P, :]).then_inc(sem_, 16)
                else:
                    for half in range(2):
                        sp.dma_start(x[half * DB:(half + 1) * DB, k, :], xT[b, JC * P:J, :]).then_inc(sem_, 16)

            def load_wt(k):
                if k < 2 * JC:
                    j0 = (k // 2) * P
                    src = wT[j0:j0 + P, :, :].rearrange("j (c q i) o -> j c q (i o)", c=2, q=2)[:, :, k % 2, :]
                    sp.dma_start(w_tok[:, k, :, :].rearrange("p (c i) o -> p c (i o)", c=2), src).then_inc(wt_in[k], 16)
                else:
                    for half in range(2):
                        src = wT[JC * P:J, :, :].rearrange("j (c f) o -> j c f o", f=2)[:, :, half, :]
                        sp.dma_start(w_tok[half * DB:(half + 1) * DB, k, :, :], src).then_inc(wt_in[k], 16)

            for half in range(2):
                sp.dma_start(f_col[half * DB:(half + 1) * DB, :],
                             freqs[half:half + 1, :].to_broadcast([DB, NF + 3])).then_inc(f_in, 16)
            load_x(0, 0)
            sp.dma_start(h_c[:, 0, :], cls_tok[0:1, :].to_broadcast([CLS, D])).then_inc(cls_in, 16)
            small(ident[:, :], consts[:, 0:P])
            small(wqk_a[:, 0, :], wq[0:P, :])
            small(wqk_a[:, 1, :], wk[0:P, :])
            small(wqk_b[:, 0, :], wq[P:D, :])
            small(wqk_b[:, 1, :], wk[P:D, :])
            for i in range(2):
                small(wff_a[:, i, :], wf[0:P, :])
                small(wff_b[:, i, :], wf[P:D, :])
                small(neg_bf[i * M:(i + 1) * M, :], bf)
            small(wv_a[:, :], wv[0:P, :])
            small(wv_b[:, :], wv[P:D, :])
            load_wt(0)
            small(wo_a[:, :], wo[0:P, :])
            small(wo_b[:, :], wo[P:D, :])
            for i, src in enumerate((gamma, beta)):
                small(gb_a[:, i:i + 1], src[0:P, :])
                small(gb_b[:, i:i + 1], src[P:D, :])
            small(causal[:, :], consts[:, P:2 * P])
            small(sgb[:, :], sg_b[0:1, :].to_broadcast([P, 1]))
            sp.dma_start(pick_raw[:, :], consts[0:GR, 2 * P:2 * P + NE + 1]).then_inc(w_small, 16)
            sp.dma_start(rank[:, :], consts[:, 2 * P + NE + 1:2 * P + 2 * NE + 1]).then_inc(w_small, 16)
            sp.wait_ge(consts_ok, 1)
            for lo, hi, half, row in ((0, P, 0, 0), (0, DB, 1, P), (DB, P, 1, P)):
                sp.dma_start(wr_raw[lo:hi, half, 0:NE], wr[row:row + hi - lo, :]).then_inc(router_hi, 16)
                sp.dma_start(wr_raw[lo:hi, half, NE:NE + 1], sg_w[row:row + hi - lo, :]).then_inc(router_hi, 16)

            def load_piece(p):
                if p >= 1:
                    sp.wait_ge(split_done, 2 * p)
                else:
                    sp.wait_ge(xpose3, 1)
                cut = slice(PC * p, PC * (p + 1))
                sp.dma_start(h2[:, :, :].rearrange("p a b -> p (a b)"),
                             wgu[0:P, cut, :].rearrange("k c n -> k (c n)")).then_inc(wgu_raw, 16)
                for half in range(2):
                    sp.dma_start(xn[half * DB:(half + 1) * DB, :, :].rearrange("p a b -> p (a b)")[:, 0:PC * 2 * P],
                                 wgu[P:D, cut, :].rearrange("k c n -> k (c n)")).then_inc(wgu_raw, 16)

            for k in range(1, NG):
                if k % 2 == 0:
                    load_x(0, x_block(k))
                load_wt(k)
                if k >= 3:
                    load_piece(k - 3)
            sp.dma_start(w_down[:, :, :], wd.rearrange("(c p) d -> p c d", p=P)).then_inc(wdown_in, 16)

            def next_x(a):
                sp.wait_ge(r_ready, NG * (a + 1))
                for k in range(JC + 1):
                    load_x(a + 1, k)

            def store(b, f):
                sp.wait_ge(out_ready, f + 1)
                sp.dma_start(out[b, 1:T + 1, :].rearrange("(i p) d -> p i d", p=P), h2[:, :, :]).then_inc(out_dma, 16)

            next_x(0)
            next_x(1)
            store(0, 0)
            for a in range(2, B - 1):
                next_x(a)
                store(a - 1, a - 1)
            store(B - 2, B - 2)
            sp.wait_ge(out_ready, B)
            for b in range(B):
                sp.dma_start(out[b, 0:1, :], h2_c[0:1, 0, :]).then_inc(clsout_dma, 16)
            store(B - 1, B)
            sp.wait_ge(out_dma, 16 * B)
            sp.wait_ge(clsout_dma, 16 * B)

        @block.gpsimd
        def _(pool):
            def rounds(a, k):
                q = NG * a + k
                if not (q < SLOTS):
                    pool.wait_ge(tok_group, q - SLOTS + 1)
                if a >= 2 and k == SLOTS - 1:
                    pool.wait_ge(down_ready, NC * (a - 1))
                if a == 0 and k == 0:
                    pool.wait_ge(f_in, 32)
                pool.wait_ge(xc_in[x_block(k)], x_parts(k) * (a + 1))
                for i in range(3):
                    fi = f_index(k, i)
                    ins = pool.tensor_scalar(feat[:, k % SLOTS, i, :], x[:, x_block(k), :], f_col[:, fi:fi + 1],
                                             MAGIC, ALU.mult, ALU.add)
                ins.then_inc(n_raw, 1)
                pool.wait_ge(n_raw, q + 1)
                pool.tensor_scalar(feat[:, k % SLOTS, 0:3, :], feat[:, k % SLOTS, 0:3, :], -MAGIC, 1.0,
                                   ALU.add, ALU.mult).then_inc(n_ready, 1)

            for a in range(B):
                for k in range(NG):
                    rounds(a, k)

        @block.scalar
        def _(act):
            def sines(a, k, halves=(0, 1)):
                q = NG * a + k
                if 0 in halves:
                    act.wait_ge(r_ready, q + 1)
                    act.activation(feat[:, k % SLOTS, 0:3, :], feat[:, k % SLOTS, 0:3, :], ACT.Sin, scale=TWO_PI)
                if 1 in halves:
                    act.activation(feat[:, k % SLOTS, 3:6, :], feat[:, k % SLOTS, 3:6, :], ACT.Sin,
                                   bias=half_pi[:, :], scale=-TWO_PI).then_inc(sin_ready, 1)

            def take_h(b):
                act.wait_ge(tok_group, NG * (b + 1))
                act.wait_ge(h2_ready, b + 1)
                for i in range(2):
                    ins = act.activation(h[:, 2 * i:2 * i + 2, :].rearrange("p a b -> p (a b)"),
                                         ps[:, TB0 + i, 0:2 * D], ACT.Copy)
                ins.then_inc(h_ready, 1)

            def attn1(a):
                W, TP, nt = width(a)
                act.wait_ge(xpose1, a + 1)
                act.activation(xt_a[:, 0:W], ps[:, A0, 0:W], ACT.Copy).then_inc(xta_ready, 1)

            def take_v(a, i):
                W, TP, nt = width(a)
                if i == 0:
                    act.wait_ge(v01_psum, a + 1)
                else:
                    act.wait_ge(v23_psum, a)
                n = min(2, nt)
                ins = act.activation(v[0:TP, 2 * i:2 * i + n, 0:D],
                                     ps[0:TP, (A1, A0)[i], 0:n * D].rearrange("p (t d) -> p t d", d=D), ACT.Copy)
                if nt == 1 or i == 1:
                    ins.then_inc(v_ready, 1)

            def odds(a):
                W, TP, nt = width(a)
                act.wait_ge(f_psum, a + 1)
                act.activation(r[:, R_S, 0:W], ps[:, A0, 0:W], ACT.Exp, bias=neg_bf[:, :],
                               scale=-1.0).then_inc(odds_ready, 1)
                act.wait_ge(e_ready, a + 1)
                act.activation(r[:, R_E, 0:W], r[:, R_E, 0:W], ACT.Exp).then_inc(ee_ready, 1)

            def log_odds(a):
                W, TP, nt = width(a)
                act.wait_ge(oddsc_ready, a + 1)
                act.activation(r[:, R_S, 0:W], r[:, R_S, 0:W], ACT.Ln, bias=one[:, :], scale=1.0).then_inc(s_ready, 1)

            def powers(a):
                W, TP, nt = width(a)
                act.wait_ge(c_ready, a + 1)
                act.activation(r[:, R_P, 0:W], r[:, R_C, 0:W], ACT.Exp, scale=p_sign[:, :]).then_inc(p_ready, 1)

            def move_k(a):
                W, TP, nt = width(a)
                act.wait_ge(qk_ready, a + 1)
                act.dma_start(r[0:M, R_K, 0:W], r[M:P, R_QK, 0:W]).then_inc(k_in, 16)

            def attn2(a):
                take_v(a, 0)
                odds(a)
                if a >= 1:
                    take_v(a, 1)
                log_odds(a)
                powers(a)
                move_k(a)

            def attn3(a):
                act.wait_ge(at_diag, a + 1)
                for j in range(NT - 1):
                    bank, c0 = score_place(j)
                    ins = act.activation(at[:, j, P:T - P * j], ps[:, bank, c0 + P:c0 + T - P * j], ACT.Copy)
                ins.then_inc(at_rest, 1)

            def attn6(a):
                W, TP, nt = width(a)
                act.wait_ge(xpose2, a + 1)
                act.activation(xt_a[:, 0:W], ps[:, A0, 0:W], ACT.Identity, bias=gb_a[:, 1:2],
                               scale=gb_a[:, 0:1]).then_inc(nta_ready, 1)

            def attn8(a):
                W, TP, nt = width(a)
                _, _, _, xh_a_, _, xh_b_, _, _ = tiles(a)
                act.wait_ge(xpose3, a + 1)
                act.activation(xh_a_[:, 0:W], ps[:, A2, 0:W], ACT.Copy)
                act.activation(xh_b_[:, 0:W], ps[:, A1, 0:W], ACT.Copy).then_inc(xh_ready, 1)

            def router(a):
                W, TP, nt = width(a)
                act.wait_ge(dz_ready, a + 1)
                act.activation(ez[0:TP, 0:nt, :], dz[0:TP, 0:nt, :], ACT.Exp).then_inc(ez_ready, 1)

            def gates(a):
                W, TP, nt = width(a)
                gate_ = tiles(a)[-1]
                act.wait_ge(gt_psum, a + 1)
                act.activation(gate_[:, 0:W], ps[0:GR, A2, 0:W], ACT.Copy).then_inc(gate_ready, 1)

            def silu(f, c, cls=False):
                q = NC * f + c
                act.wait_ge(g_psum, q + 1)
                if c >= 2:
                    act.wait_ge(t_ready, q - 1)
                if cls:
                    dst, src = act_c[:, c % 2, :], ps[:, G0, 0:CLS]
                else:
                    dst, src = fr[:, F_S + c % 2, :], ps[:, G0, :]
                act.activation(dst, src, ACT.Silu).then_inc(silu_ready, 1)

            def split_hi_piece(p):
                act.wait_ge(wgu_raw, 48 * (p + 1))
                cut = slice(PC * p, PC * (p + 1))
                act.activation(wa_hi[:, cut, :, :].rearrange("p c t n -> p (c t n)"),
                               h2[:, :, :].rearrange("p a b -> p (a b)"), ACT.Copy).then_inc(split_hi, 1)
                act.activation(wb[:, cut, :, :].rearrange("p c t n -> p (c t n)"),
                               xn[:, :, :].rearrange("p a b -> p (a b)")[:, 0:PC * 2 * P], ACT.Copy).then_inc(split_hi, 1)

            act.wait_ge(consts_ok, 1)
            sines(0, 0)
            sines(0, 1)
            attn1(0)
            sines(0, 2)
            act.wait_ge(consts_ok, 2)
            attn2(0)
            attn6(0)
            attn8(0)
            router(0)
            gates(0)
            for k in range(3, NG):
                sines(0, k)
                split_hi_piece(k - 3)
            take_h(0)

            sines(1, 0)
            sines(1, 1)
            attn1(1)
            sines(1, 2)
            attn2(1)
            sines(1, 3)
            attn3(1)
            sines(1, 4)
            sines(1, 5)
            attn6(1)
            sines(1, 6)
            sines(1, 7)
            attn8(1)
            sines(1, 8)
            router(1)
            gates(1)
            take_h(1)

            for a in range(2, B + 1):
                for c in range(NC):
                    silu(a - 2, c)
                    if c == AT_X1:
                        attn1(a)
                    if c == AT_QKV:
                        take_v(a, 0)
                    if c == AT_QKV + 1:
                        odds(a)
                    if c == AT_V23:
                        take_v(a, 1)
                    if c == AT_V23 + 1:
                        log_odds(a)
                    if c == AT_V23 + 3:
                        powers(a)
                    if c == AT_V23 + 4:
                        move_k(a)
                    if c == AT_SCORES:
                        attn3(a)
                    if a < B and c >= NC - 4:
                        sines(a, (c - NC + 4) // 2, [c % 2])
                if a == B:
                    break
                for k in range(NG):
                    if k >= 2:
                        sines(a, k)
                    if k == AT_X2:
                        attn6(a)
                    if k == AT_X3:
                        attn8(a)
                    if k == AT_LG:
                        router(a)
                    if k == AT_GT:
                        gates(a)
                take_h(a)

            for c in range(NC):
                silu(B - 1, c, cls=True)
                if c == CT_X2:
                    attn6(B)
                if c == CT_X3:
                    attn8(B)
                if c == CT_LG:
                    router(B)
                if c == CT_GT:
                    gates(B)
            for c in range(NC):
                silu(B, c)

        @block.vector
        def _(dve):
            def layernorm(src, dst, a, which, TP, nt, done, twice=False, parts=(0, 1, 2)):
                n0 = (3 * a + which) * LNS
                step = [0 if 0 in parts else 2]

                def next_(ins):
                    step[0] += 1
                    ins.then_inc(ln_step, 1)
                    dve.wait_ge(ln_step, n0 + step[0])

                if 0 in parts:
                    for i in range(nt):
                        ins = dve.bn_stats(st[0:TP, i, :], src[0:TP, i, 0:D])
                    next_(ins)
                    for i in range(nt):
                        ins = dve.bn_aggr(mv[0:TP, i, :], st[0:TP, i, :])
                    next_(ins)
                v_, y_, a_ = ve[0:TP, 0:nt], y[0:TP, 0:nt], ya[0:TP, 0:nt]
                if 1 in parts:
                    next_(dve.tensor_scalar(v_, mv[0:TP, 0:nt, 1], LN_EPS, None, ALU.add))
                    next_(dve.tensor_scalar(y_.bitcast(I32), v_.bitcast(I32), 1, None, ALU.logical_shift_right))
                    next_(dve.tensor_scalar(y_.bitcast(I32), y_.bitcast(I32), -1.0, RSQRT_SEED, ALU.mult, ALU.add))
                    for _ in range(3):
                        next_(dve.scalar_tensor_tensor(a_, y_, -0.5, y_, ALU.mult, ALU.mult))
                        next_(dve.tensor_tensor(a_, a_, v_, ALU.mult))
                        next_(dve.scalar_tensor_tensor(y_, a_, 1.5, y_, ALU.add, ALU.mult))
                if 2 in parts:
                    for i in range(nt):
                        ins = dve.tensor_scalar(dst[0:TP, i, 0:D], src[0:TP, i, 0:D], mv[0:TP, i, 0:1],
                                                y[0:TP, i:i + 1], ALU.subtract, ALU.mult)
                        if twice:
                            ins = dve.tensor_scalar(dst[0:TP, i, D:D + DB], src[0:TP, i, P:D], mv[0:TP, i, 0:1],
                                                    y[0:TP, i:i + 1], ALU.subtract, ALU.mult)
                    ins.then_inc(done, 1)

            def remainders(a, k):
                q = NG * a + k
                s = k % SLOTS
                dve.wait_ge(n_ready, q + 1)
                for i in range(3):
                    fi = f_index(k, i)
                    ins = dve.scalar_tensor_tensor(feat[:, s, i, :], x[:, x_block(k), :], f_col[:, fi:fi + 1],
                                                   feat[:, s, i, :], ALU.mult, ALU.subtract)
                ins.then_inc(r_raw, 1)
                dve.wait_ge(r_raw, q + 1)
                dve.tensor_scalar(feat[:, s, 3:6, :].bitcast(I32), feat[:, s, 0:3, :].bitcast(I32), 0x7FFFFFFF, None,
                                  ALU.bitwise_and).then_inc(r_ready, 1)

            def attn0(a, parts=(0, 1, 2)):
                W, TP, nt = width(a)
                h_, _, xn_ = tiles(a)[:3]
                if a == 0:
                    dve.wait_ge(cls_in, 16)
                elif 0 in parts:
                    dve.wait_ge(h_ready, a)
                    dve.wait_ge(xpose3, a)
                layernorm(h_, xn_, a, 0, TP, nt, xn_ready, parts=parts)

            def attn1(a):
                W, TP, nt = width(a)
                dve.wait_ge(xpose1, a + 1)
                dve.tensor_copy(xt_b[:, 0:W], ps[0:DB, A1, 0:W]).then_inc(xtb_ready, 1)

            def negatives(a):
                W, TP, nt = width(a)
                dve.wait_ge(qk_psum, a + 1)
                dve.tensor_scalar(r[:, R_E, 0:W], ps[:, A2, 0:W], 0.0, None, ALU.min).then_inc(e_ready, 1)

            def clip_odds(a):
                W, TP, nt = width(a)
                dve.wait_ge(odds_ready, a + 1)
                dve.tensor_scalar(r[:, R_S, 0:W], r[:, R_S, 0:W], MAX_ODDS, None, ALU.min).then_inc(oddsc_ready, 1)
                dve.wait_ge(ee_ready, a + 1)
                dve.scalar_tensor_tensor(r[:, R_PHI, 0:W], ps[:, A2, 0:W], 0.0, r[:, R_E, 0:W],
                                         ALU.max, ALU.add).then_inc(phi_ready, 1)

            def running_sum(a):
                W, TP, nt = width(a)
                dve.wait_ge(s_ready, a + 1)
                dve.tensor_tensor_scan(r[:, R_C, 0:W], one[:, 0:1].to_broadcast([P, W]), r[:, R_S, 0:W],
                                       0.0 if a == 0 else s_c[:, 0:1], ALU.mult, ALU.add).then_inc(scan_ready, 1)
                dve.wait_ge(scan_ready, a + 1)
                if a == 0:
                    dve.tensor_copy(s_c[:, :], r[:, R_S, 0:1])
                dve.tensor_scalar(r[:, R_C, 0:W], r[:, R_C, 0:W], CLIP, -CLIP, ALU.min, ALU.max).then_inc(c_ready, 1)

            def weigh_qk(a):
                W, TP, nt = width(a)
                dve.wait_ge(p_ready, a + 1)
                dve.wait_ge(phi_ready, a + 1)
                dve.scalar_tensor_tensor(r[:, R_QK, 0:W], r[:, R_PHI, 0:W], qk_scale[:, 0:1], r[:, R_P, 0:W],
                                         ALU.mult, ALU.mult).then_inc(qk_ready, 1)

            def attn2(a):
                negatives(a)
                clip_odds(a)
                running_sum(a)
                weigh_qk(a)

            def attn3(a):
                W, TP, nt = width(a)
                dve.wait_ge(at_psum, a + 1)
                for j in range(nt):
                    bank, c0 = score_place(j)
                    ins = dve.tensor_tensor(at[0:TP, j, 0:TP], ps[0:TP, bank, c0:c0 + TP], causal[0:TP, 0:TP],
                                            ALU.mult)
                ins.then_inc(at_diag, 1)

            def make_state():
                dve.wait_ge(state_psum, 1)
                dve.tensor_scalar(state[:, :], ps[0:M, A1, 0:D + 1], r[0:M, R_K, 0:1], None,
                                  ALU.mult).then_inc(state_ready, 1)

            def divide(a):
                W, TP, nt = width(a)
                xn_ = tiles(a)[2]
                n = min(2, nt)
                dve.wait_ge(av_psum, a + 1)
                for i in range((nt + 1) // 2):
                    ins = dve.tensor_scalar(den[0:TP, 2 * i:2 * i + n], ps[0:TP, AV_BANK[i], 0:n * (D + 1)].rearrange(
                        "p (t d) -> p t d", d=D + 1)[:, :, D], DEN_EPS, None, ALU.add)
                ins.then_inc(den_ready, 1)
                dve.wait_ge(den_ready, a + 1)
                dve.reciprocal(rden[0:TP, 0:nt], den[0:TP, 0:nt]).then_inc(rden_ready, 1)
                dve.wait_ge(rden_ready, a + 1)
                for i in range(nt):
                    c0 = (i % 2) * (D + 1)
                    ins = dve.tensor_scalar(xn_[0:TP, i, 0:D], ps[0:TP, AV_BANK[i // 2], c0:c0 + D],
                                            rden[0:TP, i:i + 1], None, ALU.mult)
                ins.then_inc(hh_ready, 1)
                dve.wait_ge(hh_ready, a + 1)

            def norm_heads(a, parts=(0, 1, 2)):
                W, TP, nt = width(a)
                xn_ = tiles(a)[2]
                layernorm(xn_, xn_, a, 1, TP, nt, hn_ready, parts=parts)

            def attn5(a):
                divide(a)
                norm_heads(a)

            def attn6(a):
                W, TP, nt = width(a)
                dve.wait_ge(xpose2, a + 1)
                dve.tensor_scalar(xt_b[:, 0:W], ps[0:DB, A2, 0:W], gb_b[:, 0:1], gb_b[:, 1:2], ALU.mult,
                                  ALU.add).then_inc(ntb_ready, 1)

            def attn7(a):
                W, TP, nt = width(a)
                h_, h2_, xn_ = tiles(a)[:3]
                dve.wait_ge(wo_psum, a + 1)
                if not (a < 2):
                    dve.wait_ge(out_dma, 16 * (a - 1))
                n = min(2, nt)
                for i in range((nt + 1) // 2):
                    ins = dve.tensor_tensor(
                        h2_[0:TP, 2 * i:2 * i + n, :], h_[0:TP, 2 * i:2 * i + n, :],
                        ps[0:TP, WO_BANK[i], 0:n * D].rearrange("p (t d) -> p t d", d=D), ALU.add)
                ins.then_inc(h2_ready, 1)
                dve.wait_ge(h2_ready, a + 1)
                layernorm(h2_, xn_, a, 2, TP, nt, xn2_ready, twice=True)

            def attn8(a):
                W, TP, nt = width(a)
                _, _, _, xh_a_, xl_a_, xh_b_, xl_b_, _ = tiles(a)
                dve.wait_ge(xh_ready, a + 1)
                dve.tensor_tensor(xl_a_[:, 0:W], ps[:, A2, 0:W], xh_a_[:, 0:W].bitcast(F32), ALU.subtract)
                dve.tensor_tensor(xl_b_[:, 0:W], ps[0:DB, A1, 0:W], xh_b_[0:DB, 0:W].bitcast(F32),
                                  ALU.subtract).then_inc(xl_ready, 1)

            TOPS = 12

            def router(a):
                W, TP, nt = width(a)
                step = [0]

                def next_(ins):
                    step[0] += 1
                    ins.then_inc(top_step, 1)
                    dve.wait_ge(top_step, TOPS * a + step[0])

                L, L2, K = lg[0:TP, 0:nt, 0:NE], lg2[0:TP, 0:nt, :], key[0:TP, 0:nt, :]
                ranks = rank[0:TP, :].unsqueeze(1).to_broadcast([TP, nt, NE])

                def wide(t):
                    return t.unsqueeze(2).to_broadcast([TP, nt, NE])

                dve.wait_ge(lg_psum, a + 1)
                next_(dve.tensor_copy(lg[0:TP, 0:nt, :], ps[0:TP, A0, 0:16 * nt].rearrange(
                    "p (t n) -> p t n", n=16)[:, :, 0:NE + 1]))
                for row, (src, oh) in enumerate(((L, oh1[0:TP, 0:nt, :]), (L2, oh2[0:TP, 0:nt, :]))):
                    best, at_ = top[0:TP, 2 * row, 0:nt], top[0:TP, 2 * row + 1, 0:nt]
                    next_(dve.tensor_reduce(best, src, AX_X, ALU.max))
                    next_(dve.tensor_tensor(K, src, wide(best), ALU.is_equal))
                    next_(dve.tensor_tensor(K, K, ranks, ALU.mult))
                    next_(dve.tensor_reduce(at_, K, AX_X, ALU.max))
                    next_(dve.tensor_tensor(oh, K, wide(at_), ALU.is_equal))
                    if row == 0:
                        next_(dve.scalar_tensor_tensor(L2, oh, -FAR, L, ALU.mult, ALU.add))
                assert step[0] == TOPS
                dve.tensor_tensor(dz[0:TP, 0:nt, 0], top[0:TP, 2, 0:nt], top[0:TP, 0, 0:nt], ALU.subtract)
                dve.tensor_scalar(dz[0:TP, 0:nt, 1], lg[0:TP, 0:nt, NE], sgb[0:TP, 0:1], -1.0, ALU.add,
                                  ALU.mult).then_inc(dz_ready, 1)
                dve.wait_ge(ez_ready, a + 1)
                gstep = [0]

                def gnext(ins):
                    gstep[0] += 1
                    ins.then_inc(gt_step, 1)
                    dve.wait_ge(gt_step, 8 * a + gstep[0])

                e, iz_ = ez[0:TP, 0:nt, :], iz[0:TP, 0:nt, :]
                gnext(dve.tensor_scalar(iz_, e, 1.0, None, ALU.add))
                gnext(dve.reciprocal(iz_, iz_))
                dve.tensor_tensor(ga[0:TP, 0:nt, 1], e[:, :, 0], iz_[:, :, 0], ALU.mult)
                gnext(dve.tensor_scalar(ga[0:TP, 0:nt, 2], iz_[:, :, 1], -1.0, 1.0, ALU.mult, ALU.add))
                dve.tensor_tensor(ga[0:TP, 0:nt, 0], iz_[:, :, 0], ga[0:TP, 0:nt, 2], ALU.mult)
                gnext(dve.tensor_tensor(ga[0:TP, 0:nt, 1], ga[0:TP, 0:nt, 1], ga[0:TP, 0:nt, 2], ALU.mult))
                dve.tensor_tensor(oh1[0:TP, 0:nt, :], oh1[0:TP, 0:nt, :], wide(ga[0:TP, 0:nt, 0]), ALU.mult)
                gnext(dve.tensor_tensor(oh2[0:TP, 0:nt, :], oh2[0:TP, 0:nt, :], wide(ga[0:TP, 0:nt, 1]), ALU.mult))
                dve.tensor_tensor(gm[0:TP, 0:nt, 0:NE], oh1[0:TP, 0:nt, :], oh2[0:TP, 0:nt, :], ALU.add)
                gnext(dve.tensor_copy(gm[0:TP, 0:nt, NE], iz_[:, :, 1]))
                gnext(dve.tensor_copy(gm_hi[0:TP, 0:nt, :], gm[0:TP, 0:nt, :]))
                dve.tensor_copy(gt[0:TP, 0:nt, 0:NE + 1], gm_hi[0:TP, 0:nt, :].bitcast(F32))
                gnext(dve.tensor_tensor(gt[0:TP, 0:nt, GLO:GR], gm[0:TP, 0:nt, :], gm_hi[0:TP, 0:nt, :].bitcast(F32),
                                        ALU.subtract))
                assert gstep[0] == 8

            def hidden(f, c, cls=False):
                q = NC * f + c
                u_, m_ = ps[:, U0, :], ps[:, M0, :]
                if cls:
                    S_, t_, hid_ = act_c[:, c % 2, :], act_c[:, 2, :], act_c[:, 3 + c % 3, :]
                    u_, m_ = u_[:, 0:CLS], m_[:, 0:CLS]
                else:
                    S_, t_, hid_ = fr[:, F_S + c % 2, :], fr[:, F_T, :], fr[:, F_H + c % 3, :]
                dve.wait_ge(u_psum, q + 1)
                dve.wait_ge(silu_ready, q + 1)
                if c >= 1:
                    dve.wait_ge(hid_ready, q)
                dve.tensor_tensor(t_, S_, u_, ALU.mult).then_inc(t_ready, 1)
                dve.wait_ge(t_ready, q + 1)
                dve.wait_ge(m_psum, q + 1)
                if c >= 3:
                    dve.wait_ge(down_ready, q - 2)
                dve.tensor_tensor(hid_, t_, m_, ALU.mult).then_inc(hid_ready, 1)

            def finish(f, cls=False):
                dve.wait_ge(down_ready, NC * (f + 1))
                if cls:
                    dve.tensor_tensor(h2_c[:, 0, :], h2_c[:, 0, :], ps[0:CLS, DN0, 0:D],
                                      ALU.add).then_inc(out_ready, 1)
                    return
                for i in range(2):
                    ins = dve.tensor_tensor(
                        h2[:, 2 * i:2 * i + 2, :], h2[:, 2 * i:2 * i + 2, :],
                        ps[:, DN0 + i, 0:2 * D].rearrange("p (t d) -> p t d", d=D), ALU.add)
                ins.then_inc(out_ready, 1)

            def split_piece(p):
                cut = slice(PC * p, PC * (p + 1))
                dve.wait_ge(split_hi, 2 * p + 2)
                dve.tensor_tensor(wa_lo[:, cut, :, :].rearrange("p c t n -> p (c t n)"),
                                  h2[:, :, :].rearrange("p a b -> p (a b)"),
                                  wa_hi[:, cut, :, :].rearrange("p c t n -> p (c t n)").bitcast(F32),
                                  ALU.subtract).then_inc(split_done, 1)
                low = wb[DB:P, cut, :, :].rearrange("p c t n -> p (c t n)")
                dve.tensor_tensor(low, xn[DB:P, :, :].rearrange("p a b -> p (a b)")[:, 0:PC * 2 * P], low.bitcast(F32),
                                  ALU.subtract).then_inc(split_done, 1)

            dve.memset(half_pi[:, :], HALF_PI)
            dve.memset(wr_raw[:, :, :], 0.0).then_inc(consts_ok, 1)
            dve.memset(one[:, :], 1.0)
            dve.memset(v[:, :, D:D + 1], 1.0)
            dve.memset(gt[:, :, :], 0.0)
            dve.memset(qk_scale[0:M, :], float(M) ** -0.5)
            dve.memset(qk_scale[M:P, :], 1.0)
            dve.memset(p_sign[0:M, :], -1.0)
            dve.memset(p_sign[M:P, :], 1.0)
            dve.wait_ge(w_small, 16 * N_SMALL)
            dve.tensor_scalar(neg_bf[:, :], neg_bf[:, :], -1.0, None, ALU.mult)
            dve.tensor_copy(pick[:, :, :], pick_raw[:, :].unsqueeze(2).to_broadcast([GR, NE + 1, P // 2])).then_inc(consts_ok, 1)
            remainders(0, 0)
            remainders(0, 1)
            dve.wait_ge(router_hi, 16 * 6)
            dve.tensor_copy(wra_hi[:, :], wr_raw[:, 0, :])
            dve.tensor_copy(wrb[:, :], wr_raw[:, 1, :]).then_inc(router_split, 1)
            dve.wait_ge(router_split, 1)
            dve.tensor_tensor(wra_lo[:, :], wr_raw[:, 0, :], wra_hi[:, :].bitcast(F32), ALU.subtract)
            dve.tensor_tensor(wrb[DB:P, :], wr_raw[DB:P, 1, :], wrb[DB:P, :].bitcast(F32),
                              ALU.subtract).then_inc(router_split, 1)
            attn0(0)
            attn1(0)
            remainders(0, 2)
            attn2(0)
            attn3(0)
            make_state()
            attn5(0)
            attn6(0)
            attn7(0)
            attn8(0)
            router(0)
            for k in range(3, NG):
                remainders(0, k)
                split_piece(k - 3)
            dve.wait_ge(split_done, 2 * PIECES)
            attn0(1)

            remainders(1, 0)
            remainders(1, 1)
            attn1(1)
            remainders(1, 2)
            attn2(1)
            remainders(1, 3)
            attn3(1)
            remainders(1, 4)
            attn5(1)
            remainders(1, 5)
            attn6(1)
            remainders(1, 6)
            attn7(1)
            remainders(1, 7)
            attn8(1)
            remainders(1, 8)
            router(1)

            for a in range(2, B + 1):
                attn0(a, [0])
                for c in range(NC):
                    hidden(a - 2, c)
                    if c < 2:
                        attn0(a, [c + 1])
                    if c == AT_X1:
                        attn1(a)
                    if c == AT_QKV:
                        negatives(a)
                    if c == AT_QKV + 2:
                        clip_odds(a)
                    if c == AT_V23 + 2:
                        running_sum(a)
                    if c == AT_V23 + 4:
                        weigh_qk(a)
                    if c == AT_SCORES:
                        attn3(a)
                    if c == AT_AV:
                        divide(a)
                    if a < B and c in AT_AHEAD:
                        remainders(a, AT_AHEAD.index(c))
                finish(a - 2)
                norm_heads(a)
                if a == B:
                    break
                for k in range(NG):
                    if k >= 2:
                        remainders(a, k)
                    if k == AT_X2:
                        attn6(a)
                    if k == AT_WO:
                        attn7(a)
                    if k == AT_X3:
                        attn8(a)
                    if k == AT_LG:
                        router(a)

            for c in range(NC):
                hidden(B - 1, c, cls=True)
                if c == CT_X2:
                    attn6(B)
                if c == CT_WO:
                    attn7(B)
                if c == CT_X3:
                    attn8(B)
                if c == CT_LG:
                    router(B)
            finish(B - 1, cls=True)
            for c in range(NC):
                hidden(B, c)
            finish(B)

        @block.tensor
        def _(pe):
            def project(a, k):
                q = NG * a + k
                if a == 0:
                    pe.wait_ge(wt_in[k], x_parts(k))
                elif k == 0:
                    pe.wait_ge(h_ready, a)
                if k == 0 and a >= 2:
                    pe.wait_ge(silu_ready, NC * (a - 1))
                    pe.wait_ge(t_ready, NC * (a - 1))
                pe.wait_ge(sin_ready, q + 1)
                for i in range(6):
                    for t in range(NT):
                        ins = pe.matmul(ps[:, TB0 + t // 2, (t % 2) * D:(t % 2 + 1) * D],
                                        feat[:, k % SLOTS, i, t * P:(t + 1) * P], w_tok[:, k, i, :],
                                        start=(k == 0 and i == 0 and t % 2 == 0), stop=(k == NG - 1 and i == 5),
                                        skip_group_check=True)
                ins.then_inc(tok_group, 1)

            def attn1(a):
                W, TP, nt = width(a)
                xn_ = tiles(a)[2]
                pe.wait_ge(xn_ready, a + 1)
                for i in range(nt):
                    pe.transpose(ps[:, A0, i * P:i * P + TP], xn_[0:TP, i, 0:P], ident[0:TP, 0:TP])
                for i in range(nt):
                    ins = pe.transpose(ps[0:DB, A1, i * P:i * P + TP], xn_[0:TP, i, P:D], ident[0:TP, 0:TP])
                ins.then_inc(xpose1, 1)

            def values(a, first):
                W, TP, nt = width(a)
                for i in range(first, min(first + 2, nt)):
                    o = ps[0:TP, (A1, A0)[i // 2], (i % 2) * D:(i % 2 + 1) * D]
                    pe.matmul(o, xt_a[:, i * P:i * P + TP], wv_a[:, :], start=True, stop=False)
                    ins = pe.matmul(o, xt_b[:, i * P:i * P + TP], wv_b[:, :], start=False, stop=True)
                ins.then_inc((v01_psum, v23_psum)[first // 2], 1)

            def attn2(a):
                W, TP, nt = width(a)
                pe.wait_ge(xta_ready, a + 1)
                pe.wait_ge(xtb_ready, a + 1)

                def pair(bank, wa, wb_):
                    pe.matmul(ps[:, bank, 0:W], wa.rearrange("k a b -> k (a b)"), xt_a[:, 0:W], start=True, stop=False)
                    return pe.matmul(ps[:, bank, 0:W], wb_.rearrange("k a b -> k (a b)"), xt_b[:, 0:W],
                                     start=False, stop=True)

                pair(A0, wff_a[:, :, :], wff_b[:, :, :]).then_inc(f_psum, 1)
                if a >= 1:
                    pe.wait_ge(gate_ready, a)
                pair(A2, wqk_a[:, :, :], wqk_b[:, :, :]).then_inc(qk_psum, 1)
                values(a, 0)

            def attn2b(a):
                pe.wait_ge(odds_ready, a + 1)
                values(a, 2)

            def attn3(a):
                W, TP, nt = width(a)
                pe.wait_ge(k_in, 16 * (a + 1))
                pe.wait_ge(qk_ready, a + 1)
                pe.wait_ge(v_ready, a + 1)
                for j in range(nt):
                    bank, c0 = score_place(j)
                    ins = pe.matmul(ps[0:TP, bank, c0:c0 + W - P * j], r[0:M, R_K, j * P:j * P + TP],
                                    r[0:M, R_QK, j * P:W], start=True, stop=True)
                ins.then_inc(at_psum, 1)

            def attn5(a):
                W, TP, nt = width(a)
                if a == 0:
                    pe.matmul(ps[0:M, A1, 0:D + 1], causal[0:1, 0:M], v[0:1, 0, :], start=True,
                              stop=True).then_inc(state_psum, 1)
                pe.wait_ge(at_diag, a + 1)
                if a >= 1:
                    pe.wait_ge(at_rest, a)
                    pe.wait_ge(state_ready, 1)
                for i in range(nt):
                    o = ps[0:TP, AV_BANK[i // 2], (i % 2) * (D + 1):(i % 2 + 1) * (D + 1)]
                    if a >= 1:
                        pe.matmul(o, r[0:M, R_QK, i * P:(i + 1) * P], state[:, :], start=(i % 2 == 0), stop=False,
                                  skip_group_check=True)
                    for j in range(i + 1):
                        ins = pe.matmul(o, at[0:TP, j, (i - j) * P:(i - j) * P + TP], v[0:TP, j, :],
                                        start=(nt == 1), stop=(j == i), skip_group_check=True)
                ins.then_inc(av_psum, 1)

            def attn6(a):
                W, TP, nt = width(a)
                xn_ = tiles(a)[2]
                pe.wait_ge(hn_ready, a + 1)
                for i in range(nt):
                    pe.transpose(ps[:, A0, i * P:i * P + TP], xn_[0:TP, i, 0:P], ident[0:TP, 0:TP])
                for i in range(nt):
                    ins = pe.transpose(ps[0:DB, A2, i * P:i * P + TP], xn_[0:TP, i, P:D], ident[0:TP, 0:TP])
                ins.then_inc(xpose2, 1)

            def attn7(a):
                W, TP, nt = width(a)
                pe.wait_ge(nta_ready, a + 1)
                pe.wait_ge(ntb_ready, a + 1)
                for i in range(nt):
                    o = ps[0:TP, WO_BANK[i // 2], (i % 2) * D:(i % 2 + 1) * D]
                    pe.matmul(o, xt_a[:, i * P:i * P + TP], wo_a[:, :], start=True, stop=False)
                    ins = pe.matmul(o, xt_b[:, i * P:i * P + TP], wo_b[:, :], start=False, stop=True)
                ins.then_inc(wo_psum, 1)

            def attn8(a):
                W, TP, nt = width(a)
                xn_ = tiles(a)[2]
                pe.wait_ge(xn2_ready, a + 1)
                for i in range(nt):
                    pe.transpose(ps[:, A2, i * P:i * P + TP], xn_[0:TP, i, 0:P], ident[0:TP, 0:TP])
                for i in range(nt):
                    ins = pe.transpose(ps[:, A1, i * P:i * P + TP], xn_[0:TP, i, P:D + DB], ident[0:TP, 0:TP])
                ins.then_inc(xpose3, 1)

            def router(a):
                W, TP, nt = width(a)
                _, _, _, xh_a_, xl_a_, xh_b_, xl_b_, _ = tiles(a)
                pe.wait_ge(xh_ready, a + 1)
                pe.wait_ge(xl_ready, a + 1)
                for i in range(nt):
                    o, c = ps[0:TP, A0, 16 * i:16 * i + NR], slice(i * P, i * P + TP)
                    pe.matmul(o, xh_a_[:, c], wra_hi[:, :], start=True, stop=False)
                    pe.matmul(o, xh_a_[:, c], wra_lo[:, :], start=False, stop=False)
                    pe.matmul(o, xl_a_[:, c], wra_hi[:, :], start=False, stop=False)
                    pe.matmul(o, xh_b_[:, c], wrb[:, :], start=False, stop=False)
                    ins = pe.matmul(o, xl_b_[:, c], wrb[0:DB, :], start=False, stop=True)
                ins.then_inc(lg_psum, 1)

            def gates(a):
                W, TP, nt = width(a)
                pe.wait_ge(gt_step, 8 * (a + 1))
                for i in range(nt):
                    ins = pe.transpose(ps[0:GR, A2, i * P:i * P + TP], gt[0:TP, i, :], ident[0:TP, 0:TP])
                ins.then_inc(gt_psum, 1)

            def up(f, c, cls=False):
                q = NC * f + c
                if cls:
                    xh, xl, yh, yl, gate_ = xhc_a, xlc_a, xhc_b, xlc_b, gatec_t
                else:
                    xh, xl, yh, yl, gate_ = xh_a, xl_a, xh_b, xl_b, gate_t
                outs = [ps[:, bank, 0:CLS if cls else T] for bank in (G0, U0, M0)]
                for i, done in enumerate((g_psum, u_psum)):
                    o = outs[i]
                    if q >= 1:
                        pe.wait_ge((silu_ready, t_ready)[i], q)
                    pe.matmul(o, wa_hi[:, c, i, :], xh[:, :], start=True, stop=False)
                    pe.matmul(o, wa_lo[:, c, i, :], xh[:, :], start=False, stop=False)
                    pe.matmul(o, wa_hi[:, c, i, :], xl[:, :], start=False, stop=False)
                    pe.matmul(o, wb[:, c, i, :], yh[:, :], start=False, stop=False)
                    pe.matmul(o, wb[0:DB, c, i, :], yl[:, :], start=False, stop=True).then_inc(done, 1)
                if q >= 1:
                    pe.wait_ge(hid_ready, q)
                e0 = NE if c < NCS else (c - NCS) * P // D
                e1 = NE if c < NCS else ((c - NCS) * P + P - 1) // D
                sel = (pick[:, e0, 0:1].to_broadcast([GR, P]) if e0 == e1 else
                       pick[:, e0:e0 + 2, :].rearrange("k e m -> k (e m)"))
                pe.matmul(outs[2], sel, gate_[:, :], start=True, stop=True).then_inc(m_psum, 1)

            def down(f, c, cls=False):
                q = NC * f + c
                pe.wait_ge(hid_ready, q + 1)
                if c == 0 and f >= 1:
                    pe.wait_ge(out_ready, f)
                for t in range(1 if cls else NT):
                    if cls:
                        o, hid = ps[0:CLS, DN0, 0:D], act_c[:, 3 + c % 3, :]
                    else:
                        o, hid = ps[:, DN0 + t // 2, (t % 2) * D:(t % 2 + 1) * D], fr[:, F_H + c % 3, t * P:(t + 1) * P]
                    ins = pe.matmul(o, hid, w_down[:, c, :], start=(c == 0 and t % 2 == 0), stop=(c == NC - 1),
                                    skip_group_check=True)
                ins.then_inc(down_ready, 1)

            def ffn_step(f, c, cls=False):
                if c < NC:
                    up(f, c, cls)
                if c >= 1:
                    down(f, c - 1, cls)

            pe.wait_ge(w_small, 16 * N_SMALL)
            attn1(0)
            project(0, 0)
            pe.wait_ge(consts_ok, 2)
            attn2(0)
            project(0, 1)
            attn3(0)
            attn5(0)
            attn6(0)
            project(0, 2)
            attn7(0)
            attn8(0)
            pe.wait_ge(router_split, 2)
            router(0)
            gates(0)
            for k in range(3, NG):
                project(0, k)

            pe.wait_ge(split_done, 2 * PIECES)
            pe.wait_ge(wdown_in, 16)

            attn1(1)
            project(1, 0)
            attn2(1)
            project(1, 1)
            attn2b(1)
            project(1, 2)
            attn3(1)
            project(1, 3)
            attn5(1)
            project(1, 4)
            attn6(1)
            project(1, 5)
            attn7(1)
            project(1, 6)
            attn8(1)
            project(1, 7)
            router(1)
            project(1, 8)
            gates(1)

            for a in range(2, B + 1):
                if a <= B:
                    pe.wait_ge(h_ready, a)
                pe.wait_ge(gate_ready, a)
                for c in range(NC + 1):
                    if c == AT_X1:
                        attn1(a)
                    if c == AT_QKV:
                        attn2(a)
                    if c == AT_V23:
                        attn2b(a)
                    if c == AT_SCORES:
                        attn3(a)
                    if c == AT_AV:
                        attn5(a)
                    ffn_step(a - 2, c)
                if a == B:
                    break
                for k in range(NG):
                    if k == AT_X2:
                        attn6(a)
                    if k == AT_WO:
                        attn7(a)
                    if k == AT_X3:
                        attn8(a)
                    if k == AT_LG:
                        router(a)
                    if k == AT_GT:
                        gates(a)
                    project(a, k)

            for c in range(NC + 1):
                if c == CT_X2:
                    attn6(B)
                if c == CT_WO:
                    attn7(B)
                if c == CT_X3:
                    attn8(B)
                if c == CT_LG:
                    router(B)
                if c == CT_GT:
                    gates(B)
                ffn_step(B - 1, c, cls=True)
            pe.wait_ge(gate_ready, B + 1)
            for c in range(NC + 1):
                ffn_step(B, c)


def kernel(x, cls_tok, L0_tok_freq_bands, L0_tok_W, L0_attn_Wq, L0_attn_Wk, L0_attn_Wv, L0_attn_Wf, L0_attn_bf,
           L0_attn_Wo, L0_attn_gamma, L0_attn_beta, L0_ffn_router_w, L0_ffn_w_gate, L0_ffn_w_up, L0_ffn_w_down,
           L0_ffn_ws_gate, L0_ffn_ws_up, L0_ffn_ws_down, L0_ffn_sg_w, L0_ffn_sg_b):
    import concourse.bacc as bacc
    from concourse.bass_utils import run_bass_kernel_spmd

    def experts(w):
        return np.asarray(w).transpose(1, 0, 2).reshape(D, NE * D)

    gate = np.concatenate([np.asarray(L0_ffn_ws_gate), experts(L0_ffn_w_gate)], axis=1)
    up = np.concatenate([np.asarray(L0_ffn_ws_up), experts(L0_ffn_w_up)], axis=1)
    consts = np.zeros((P, 2 * P + 2 * NE + 1), np.float32)
    consts[:, 0:P] = np.eye(P, dtype=np.float32)
    consts[:, P:2 * P] = np.triu(np.ones((P, P), np.float32))
    for e in range(NE + 1):
        consts[e, 2 * P + e] = consts[GLO + e, 2 * P + e] = 1.0
    consts[:, 2 * P + NE + 1:] = np.arange(NE, 0, -1, dtype=np.float32)
    fr = np.asarray(L0_tok_freq_bands)
    arrays = {
        "xT": np.asarray(x).reshape(B, T, J).transpose(0, 2, 1),
        "wT": np.asarray(L0_tok_W).reshape(D, J, 2 * NF).transpose(1, 2, 0),
        "freqs": np.stack([np.concatenate([fr, fr[half::2]]) for half in range(2)]),
        "cls_tok": np.asarray(cls_tok).reshape(1, D),
        "wq": L0_attn_Wq, "wk": L0_attn_Wk, "wv": L0_attn_Wv, "wf": L0_attn_Wf,
        "bf": np.asarray(L0_attn_bf).reshape(M, 1),
        "gamma": np.asarray(L0_attn_gamma).reshape(D, 1),
        "beta": np.asarray(L0_attn_beta).reshape(D, 1),
        "wo": L0_attn_Wo, "wr": L0_ffn_router_w, "sg_w": L0_ffn_sg_w,
        "sg_b": np.asarray(L0_ffn_sg_b).reshape(1, 1),
        "wgu": np.stack([gate.reshape(D, NC, P), up.reshape(D, NC, P)], axis=2).reshape(D, NC, 2 * P),
        "wd": np.concatenate([np.asarray(L0_ffn_ws_down), np.asarray(L0_ffn_w_down).reshape(NE * D, D)], axis=0),
        "consts": consts,
    }
    arrays = {n: np.ascontiguousarray(a) for n, a in arrays.items()}
    nc = bacc.Bacc("TRN2", target_bir_lowering=False, num_devices=1)
    args = [nc.dram_tensor(f"in_{n}", a.shape, mybir.dt.from_np(a.dtype), kind="ExternalInput").ap()
            for n, a in arrays.items()]
    out = nc.dram_tensor("out", (B, T + 1, D), F32, kind="ExternalOutput").ap()
    build(nc, *args, out)
    res = run_bass_kernel_spmd(nc, [{f"in_{n}": a for n, a in arrays.items()}], core_ids=[0])
    return res.results[0]["out"]
```

```python
from contextlib import ExitStack

import numpy as np

import concourse.bass as bass
from concourse import mybir

F32 = mybir.dt.float32
F32R = mybir.dt.float32r
I32 = mybir.dt.int32
ALU = mybir.AluOpType
ACT = mybir.ActivationFunctionType
AX_X = mybir.AxisListType.X

P = 128
B = 4
C3 = 3
T = 512
D = 192
DB = D - P
NF = 6
M = 64
NE = 8
HS = 768
HID = HS + NE * D
NC = HID // P
NCS = HS // P
NT = T // P
J = C3 * D
JC = J // P
NG = 2 * JC + 1
SLOTS = 3
CLS = 2
NR = NE + 2
GLO = 32
GR = GLO + NE + 1
PIECES = 6
PC = NC // PIECES
LNS = 14
MAGIC = 1.5 * 2.0 ** 23
RSQRT_SEED = float(0x5F3759DF)
TWO_PI = float(np.float32(2.0 * np.pi))
HALF_PI = float(np.float32(0.5 * np.pi))
LN_EPS = 1e-5
DEN_EPS = 1e-6
MAX_ODDS = float(np.float32(1e6) - np.float32(1.0))
CLIP = 20.0
FAR = 1e30
TB0, G0, U0, M0, DN0, A0, A1, A2 = 0, 0, 1, 2, 3, 5, 6, 7
AT_X1, AT_QKV, AT_V23, AT_SCORES, AT_AV, AT_X2 = 2, 3, 4, 8, 9, 12
TK_WO, TK_X3, TK_LG, TK_GT = 1, 3, 4, 6
LT_WO, LT_X3, LT_LG = 13, 16, 17
AT_AHEAD = (13, 15)
CR = 6
ROUND_BANKS = ((A1, A0, A2), (A1, A0, A2), (G0, U0, A1))
UM = 16
AV_BANK, WO_BANK = (A2, A1), (A1, A0)


PACK = {}
for name_, cols_ in (("ident", P), ("causal", P), ("qk_a", 2 * M), ("qk_b", 2 * M), ("ff_a", 2 * M), ("ff_b", 2 * M),
                     ("v_a", D), ("v_b", D), ("neg_bf", 1), ("gb_a", 2), ("gb_b", 2), ("wr", 2 * NR), ("sgb", 1),
                     ("pick", NE + 1), ("rank", NE), ("o_a", D), ("o_b", D)):
    PACK[name_] = (sum(n for _, n in PACK.values()), cols_)
PACKED = sum(n for _, n in PACK.values())


def build(nc, xT, wT, freqs, cls_tok, packed, wgu, wd, out):
    with ExitStack() as ctx:
        def sb(name, shape, dt=F32):
            return ctx.enter_context(nc.sbuf_tensor(name, shape, dt))

        def sem(name):
            return ctx.enter_context(nc.semaphore(name))

        w_tok = sb("w_tok", [P, NG, 2 * 3, D])
        wa_hi = sb("wa_hi", [P, NC, 2, P], F32R)
        wa_lo = sb("wa_lo", [P, NC, 2, P], F32R)
        wb = sb("wb", [P, NC, 2, P], F32R)
        w_down = sb("w_down", [P, NC, D])
        pack = sb("pack", [P, PACKED])

        def part(name, lo=0, hi=P):
            c0, n = PACK[name]
            return pack[lo:hi, c0:c0 + n]

        wqk_a, wff_a, wv_a, wo_a, gb_a = (part(n) for n in ("qk_a", "ff_a", "v_a", "o_a", "gb_a"))
        wqk_b, wff_b, wv_b, wo_b = (part(n, DB, P) for n in ("qk_b", "ff_b", "v_b", "o_b"))
        gb_b, neg_bf, sgb = part("gb_b", 0, DB), part("neg_bf"), part("sgb")
        ident, causal, pick_raw = part("ident"), part("causal"), part("pick", 0, GR)
        rank = part("rank")
        wr_raw = part("wr").rearrange("p (h n) -> p h n", h=2)
        wra_hi, wra_lo, wrb = (sb(n, [P, NR], F32R) for n in ("wra_hi", "wra_lo", "wrb"))
        f_col = sb("f_col", [P, NF + 3])
        qk_scale, p_sign = sb("qk_scale", [P, 1]), sb("p_sign", [P, 1])
        half_pi, warm = sb("half_pi", [P, 1]), sb("warm", [P, 1])
        pick = sb("pick", [GR, NE + 1, P // 2], F32R)
        one = sb("one", [P, 1])
        with nc.sbuf_tensor("x", [P, JC + 1, T], F32) as x:
            pass
        last = sb("last", [P, JC + 1, T], F32R)
        feat = sb("feat", [P, SLOTS, 6, T])
        h, h2 = sb("h", [P, NT, D]), sb("h2", [P, NT, D])
        xn = sb("xn", [P, NT, D + DB])
        xt_a = sb("xt_a", [P, T])
        v = sb("v", [P, NT, D + 1])
        r = sb("r", [P, 7, T])
        xh_a, xl_a = sb("xh_a", [P, T], F32R), sb("xl_a", [P, T], F32R)
        xh_b, xl_b = sb("xh_b", [P, T], F32R), sb("xl_b", [DB, T], F32R)
        gate_t = sb("gate_t", [GR, T], F32R)
        h_c = h[0:CLS, 0:1, :]
        xn_c = sb("xn_c", [CLS, 1, D + DB])
        h2_c = sb("h2_c", [CLS, 1, D])
        state = sb("state", [M, D + 1])
        s_c = sb("s_c", [P, 1])
        xhc_a, xlc_a = sb("xhc_a", [P, CLS], F32R), sb("xlc_a", [P, CLS], F32R)
        xhc_b, xlc_b = sb("xhc_b", [P, CLS], F32R), sb("xlc_b", [DB, CLS], F32R)
        gatec_t = sb("gatec_t", [GR, CLS], F32R)
        act_c = sb("act_c", [P, 3, CR * CLS])
        st, mv = sb("st", [P, NT, 6]), sb("mv", [P, NT, 2])
        ve, y, ya = sb("ve", [P, NT]), sb("y", [P, NT]), sb("ya", [P, NT])
        den, rden = sb("den", [P, NT]), sb("rden", [P, NT])
        lg, lg2 = sb("lg", [P, NT, NE + 1]), sb("lg2", [P, NT, NE])
        top = sb("top", [P, 4, NT])
        oh1, oh2, key = sb("oh1", [P, NT, NE]), sb("oh2", [P, NT, NE]), sb("key", [P, NT, NE])
        dz, ez, iz = sb("dz", [P, NT, 2]), sb("ez", [P, NT, 2]), sb("iz", [P, NT, 2])
        ga = sb("ga", [P, NT, 3])
        gm = sb("gm", [P, NT, NE + 1])
        gm_hi = sb("gm_hi", [P, NT, NE + 1], F32R)
        gt = sb("gt", [P, NT, GR])

        ps = ctx.enter_context(nc.psum_tensor("ps", [P, 8, 512], F32))

        R_E, R_PHI, R_S, R_P, R_C, R_QK, R_K = range(7)
        at = r[:, 0:4, :]
        xt_b = r[DB:P, R_K, :]
        fr = feat[:, SLOTS - 1, :, :]
        F_S, F_T, F_H = 0, 2, 3

        names = """w_small f_in wgu_raw wdown_in cls_in split_hi split_done router_split consts_ok
            n_raw n_ready r_raw r_ready sin_ready tok_group
            h_ready ln_step xn_ready xpose1 xta_ready xtb_ready qk_psum f_psum v01_psum v23_psum v_ready
            e_ready ee_ready odds_ready oddsc_ready s_ready scan_ready c_ready p_ready phi_ready
            qk_ready k_in at_psum at_diag at_rest state_psum state_ready av_psum den_ready rden_ready hh_ready hn_ready
            xpose2 nta_ready ntb_ready wo_psum h2_ready xn2_ready xpose3 xh_ready xl_ready
            lg_psum top_step dz_ready ez_ready gt_step gt_psum gate_ready
            g_psum u_psum m_psum silu_ready t_ready hid_ready down_ready out_ready out_dma
            gc_psum umc_psum siluc_ready tc_ready hidc_ready downc_ready outc_ready clsout_dma"""
        S = {n: sem(n) for n in names.split()}
        (w_small, f_in, wgu_raw, wdown_in, cls_in, split_hi, split_done, router_split, consts_ok,
         n_raw, n_ready, r_raw, r_ready, sin_ready, tok_group,
         h_ready, ln_step, xn_ready, xpose1, xta_ready, xtb_ready, qk_psum, f_psum, v01_psum, v23_psum, v_ready,
         e_ready, ee_ready, odds_ready, oddsc_ready, s_ready, scan_ready, c_ready, p_ready, phi_ready,
         qk_ready, k_in, at_psum, at_diag, at_rest, state_psum, state_ready, av_psum, den_ready, rden_ready, hh_ready, hn_ready,
         xpose2, nta_ready, ntb_ready, wo_psum, h2_ready, xn2_ready, xpose3, xh_ready, xl_ready,
         lg_psum, top_step, dz_ready, ez_ready, gt_step, gt_psum, gate_ready,
         g_psum, u_psum, m_psum, silu_ready, t_ready, hid_ready, down_ready, out_ready, out_dma,
         gc_psum, umc_psum, siluc_ready, tc_ready, hidc_ready, downc_ready, outc_ready, clsout_dma) = (S[n] for n in names.split())
        wt_in = [sem(f"wt_in{k}") for k in range(NG)]
        xc_in = [sem(f"xc_in{k}") for k in range(JC + 1)]

        def width(a):
            cls = a == 0
            return (CLS, CLS, 1) if cls else (T, P, NT)

        def tiles(a):
            if a == 0:
                return h_c, h2_c, xn_c, xhc_a, xlc_a, xhc_b, xlc_b, gatec_t
            if a == B:
                return h, h, xn, last[:, 0, :], last[:, 1, :], last[:, 2, :], last[0:DB, 3, :], last[0:GR, 4, :]
            return h, h2, xn, xh_a, xl_a, xh_b, xl_b, gate_t

        def score_place(j):
            return ((A2, 0), (A1, 0), (A0, 0), (A0, 2 * P))[j]

        def x_block(k):
            return k // 2 if k < 2 * JC else JC

        def x_parts(k):
            return 16 if k < 2 * JC else 32

        def f_index(k, i):
            return 3 * (k % 2) + i if k < 2 * JC else NF + i

        block = ctx.enter_context(nc.Block())

        @block.sync
        def _(sp):
            def load_x(b, k):
                sem_ = xc_in[k]
                if k < JC:
                    sp.dma_start(x[:, k, :], xT[b, k * P:(k + 1) * P, :]).then_inc(sem_, 16)
                else:
                    for half in range(2):
                        sp.dma_start(x[half * DB:(half + 1) * DB, k, :], xT[b, JC * P:J, :]).then_inc(sem_, 16)

            def load_wt(k):
                if k < 2 * JC:
                    j0 = (k // 2) * P
                    src = wT[j0:j0 + P, :, :].rearrange("j (c q i) o -> j c q (i o)", c=2, q=2)[:, :, k % 2, :]
                    sp.dma_start(w_tok[:, k, :, :].rearrange("p (c i) o -> p c (i o)", c=2), src).then_inc(wt_in[k], 16)
                else:
                    for half in range(2):
                        src = wT[JC * P:J, :, :].rearrange("j (c f) o -> j c f o", f=2)[:, :, half, :]
                        sp.dma_start(w_tok[half * DB:(half + 1) * DB, k, :, :], src).then_inc(wt_in[k], 16)

            for half in range(2):
                sp.dma_start(f_col[half * DB:(half + 1) * DB, :],
                             freqs[half:half + 1, :].to_broadcast([DB, NF + 3])).then_inc(f_in, 16)
            load_x(0, 0)
            load_wt(0)
            sp.dma_start(h_c[:, 0, :], cls_tok[0:1, :].to_broadcast([CLS, D])).then_inc(cls_in, 16)
            load_wt(1)
            sp.dma_start(pack[:, :], packed).then_inc(w_small, 16)

            def load_piece(p):
                if p >= 1:
                    sp.wait_ge(split_done, 2 * p)
                cut = slice(PC * p, PC * (p + 1))
                sp.dma_start(h2[:, :, :].rearrange("p a b -> p (a b)"),
                             wgu[0:P, cut, :].rearrange("k c n -> k (c n)")).then_inc(wgu_raw, 16)
                for half in range(2):
                    sp.dma_start(xn[half * DB:(half + 1) * DB, :, :].rearrange("p a b -> p (a b)")[:, 0:PC * 2 * P],
                                 wgu[P:D, cut, :].rearrange("k c n -> k (c n)")).then_inc(wgu_raw, 16)

            for k in range(2, NG):
                if k % 2 == 0:
                    load_x(0, x_block(k))
                load_wt(k)
            for p in range(PIECES):
                load_piece(p)
            sp.dma_start(w_down[:, :, :], wd.rearrange("(c p) d -> p c d", p=P)).then_inc(wdown_in, 16)

            def next_x(a):
                sp.wait_ge(r_ready, NG * (a + 1))
                for k in range(JC + 1):
                    load_x(a + 1, k)

            def store(b):
                sp.wait_ge(out_ready, b + 1)
                sp.dma_start(out[b, 1:T + 1, :].rearrange("(i p) d -> p i d", p=P), tiles(b + 1)[1][:, :, :]).then_inc(out_dma, 16)

            next_x(0)
            next_x(1)
            store(0)
            for a in range(2, B - 1):
                next_x(a)
                store(a - 1)
            store(B - 2)
            sp.wait_ge(outc_ready, NC // CR)
            for b in range(B):
                sp.dma_start(out[b, 0:1, :], h2_c[0:1, 0, :]).then_inc(clsout_dma, 16)
            store(B - 1)
            sp.wait_ge(out_dma, 16 * B)
            sp.wait_ge(clsout_dma, 16 * B)

        @block.gpsimd
        def _(pool):
            def rounds(a, k):
                q = NG * a + k
                if not (q < SLOTS):
                    pool.wait_ge(tok_group, q - SLOTS + 1)
                if a >= 2 and k == SLOTS - 1:
                    pool.wait_ge(down_ready, NC * (a - 1))
                if a == 0 and k == 0:
                    pool.wait_ge(f_in, 32)
                pool.wait_ge(xc_in[x_block(k)], x_parts(k) * (a + 1))
                for i in range(3):
                    fi = f_index(k, i)
                    ins = pool.tensor_scalar(feat[:, k % SLOTS, i, :], x[:, x_block(k), :], f_col[:, fi:fi + 1],
                                             MAGIC, ALU.mult, ALU.add)
                ins.then_inc(n_raw, 1)
                pool.wait_ge(n_raw, q + 1)
                pool.tensor_scalar(feat[:, k % SLOTS, 0:3, :], feat[:, k % SLOTS, 0:3, :], -MAGIC, 1.0,
                                   ALU.add, ALU.mult).then_inc(n_ready, 1)

            for a in range(B):
                for k in range(NG):
                    rounds(a, k)

        @block.scalar
        def _(act):
            def sines(a, k, halves=(0, 1)):
                q = NG * a + k
                if 0 in halves:
                    act.wait_ge(r_ready, q + 1)
                    act.activation(feat[:, k % SLOTS, 0:3, :], feat[:, k % SLOTS, 0:3, :], ACT.Sin,
                                   scale=TWO_PI).then_inc(sin_ready, 1)
                if 1 in halves:
                    act.activation(feat[:, k % SLOTS, 3:6, :], feat[:, k % SLOTS, 3:6, :], ACT.Sin,
                                   bias=half_pi[:, :], scale=-TWO_PI).then_inc(sin_ready, 1)

            def take_h(b):
                act.wait_ge(tok_group, NG * (b + 1))
                act.wait_ge(h2_ready, b + 1)
                for i in range(2):
                    ins = act.activation(h[:, 2 * i:2 * i + 2, :].rearrange("p a b -> p (a b)"),
                                         ps[:, TB0 + i, 0:2 * D], ACT.Copy)
                ins.then_inc(h_ready, 1)

            def attn1(a):
                W, TP, nt = width(a)
                act.wait_ge(xpose1, a + 1)
                act.activation(xt_a[:, 0:W], ps[:, A0, 0:W], ACT.Copy).then_inc(xta_ready, 1)

            def take_v(a, i):
                W, TP, nt = width(a)
                if i == 0:
                    act.wait_ge(v01_psum, a + 1)
                else:
                    act.wait_ge(v23_psum, a)
                n = min(2, nt)
                ins = act.activation(v[0:TP, 2 * i:2 * i + n, 0:D],
                                     ps[0:TP, (A1, A0)[i], 0:n * D].rearrange("p (t d) -> p t d", d=D), ACT.Copy)
                if nt == 1 or i == 1:
                    ins.then_inc(v_ready, 1)

            def odds(a):
                W, TP, nt = width(a)
                act.wait_ge(f_psum, a + 1)
                act.activation(r[:, R_S, 0:W], ps[:, A0, 0:W], ACT.Exp, bias=neg_bf[:, :],
                               scale=-1.0).then_inc(odds_ready, 1)
                act.wait_ge(e_ready, a + 1)
                act.activation(r[:, R_E, 0:W], r[:, R_E, 0:W], ACT.Exp).then_inc(ee_ready, 1)

            def log_odds(a):
                W, TP, nt = width(a)
                act.wait_ge(oddsc_ready, a + 1)
                act.activation(r[:, R_S, 0:W], r[:, R_S, 0:W], ACT.Ln, bias=one[:, :], scale=1.0).then_inc(s_ready, 1)

            def powers(a):
                W, TP, nt = width(a)
                act.wait_ge(c_ready, a + 1)
                act.activation(r[:, R_P, 0:W], r[:, R_C, 0:W], ACT.Exp, scale=p_sign[:, :]).then_inc(p_ready, 1)

            def move_k(a):
                W, TP, nt = width(a)
                act.wait_ge(qk_ready, a + 1)
                act.dma_start(r[0:M, R_K, 0:W], r[M:P, R_QK, 0:W]).then_inc(k_in, 16)

            def attn2(a):
                take_v(a, 0)
                odds(a)
                if a >= 1:
                    take_v(a, 1)
                log_odds(a)
                powers(a)
                move_k(a)

            def attn3(a):
                act.wait_ge(at_diag, a + 1)
                for j in range(NT - 1):
                    bank, c0 = score_place(j)
                    ins = act.activation(at[:, j, P:T - P * j], ps[:, bank, c0 + P:c0 + T - P * j], ACT.Copy)
                ins.then_inc(at_rest, 1)

            def attn6(a):
                W, TP, nt = width(a)
                act.wait_ge(xpose2, a + 1)
                act.activation(xt_a[:, 0:W], ps[:, A0, 0:W], ACT.Identity, bias=gb_a[:, 1:2],
                               scale=gb_a[:, 0:1]).then_inc(nta_ready, 1)

            def attn8(a):
                W, TP, nt = width(a)
                _, _, _, xh_a_, _, xh_b_, _, _ = tiles(a)
                act.wait_ge(xpose3, a + 1)
                act.activation(xh_a_[:, 0:W], ps[:, A2, 0:W], ACT.Copy)
                act.activation(xh_b_[:, 0:W], ps[:, A1, 0:W], ACT.Copy).then_inc(xh_ready, 1)

            def router(a):
                W, TP, nt = width(a)
                act.wait_ge(dz_ready, a + 1)
                act.activation(ez[0:TP, 0:nt, :], dz[0:TP, 0:nt, :], ACT.Exp).then_inc(ez_ready, 1)

            def gates(a):
                W, TP, nt = width(a)
                gate_ = tiles(a)[-1]
                act.wait_ge(gt_psum, a + 1)
                act.activation(gate_[:, 0:W], ps[0:GR, A2, 0:W], ACT.Copy).then_inc(gate_ready, 1)

            def silu(f, c):
                q = NC * f + c
                act.wait_ge(g_psum, q + 1)
                if c >= 2:
                    act.wait_ge(t_ready, q - 1)
                act.activation(fr[:, F_S + c % 2, :], ps[:, G0, :], ACT.Silu).then_inc(silu_ready, 1)

            def cls_silu(n):
                act.wait_ge(gc_psum, n + 1)
                if n >= 1:
                    act.wait_ge(tc_ready, n)
                act.activation(act_c[:, 0, :], ps[:, ROUND_BANKS[n][0], 0:CR * CLS], ACT.Silu).then_inc(siluc_ready, 1)

            def split_hi_piece(p):
                act.wait_ge(wgu_raw, 48 * (p + 1))
                cut = slice(PC * p, PC * (p + 1))
                act.activation(wa_hi[:, cut, :, :].rearrange("p c t n -> p (c t n)"),
                               h2[:, :, :].rearrange("p a b -> p (a b)"), ACT.Copy).then_inc(split_hi, 1)
                act.activation(wb[:, cut, :, :].rearrange("p c t n -> p (c t n)"),
                               xn[:, :, :].rearrange("p a b -> p (a b)")[:, 0:PC * 2 * P], ACT.Copy).then_inc(split_hi, 1)

            act.wait_ge(consts_ok, 1)
            act.activation(warm[:, :], half_pi[:, :], ACT.Sin)
            sines(0, 0)
            sines(0, 1)
            sines(0, 2)
            attn1(0)
            sines(0, 3)
            act.wait_ge(consts_ok, 2)
            attn2(0)
            sines(0, 4)
            split_hi_piece(0)
            sines(0, 5)
            attn6(0)
            split_hi_piece(1)
            sines(0, 6)
            split_hi_piece(2)
            sines(0, 7)
            attn8(0)
            split_hi_piece(3)
            sines(0, 8)
            router(0)
            split_hi_piece(4)
            gates(0)
            split_hi_piece(5)
            take_h(0)

            sines(1, 0)
            sines(1, 1)
            sines(1, 2)
            attn1(1)
            sines(1, 3)
            odds(1)
            take_v(1, 0)
            sines(1, 4)
            take_v(1, 1)
            log_odds(1)
            powers(1)
            move_k(1)
            sines(1, 5)
            attn3(1)
            sines(1, 6)
            sines(1, 7)
            attn6(1)
            sines(1, 8)
            attn8(1)
            router(1)
            gates(1)
            take_h(1)
            cls_silu(0)

            for a in range(2, B + 1):
                for c in range(NC):
                    silu(a - 2, c)
                    if c == AT_X1:
                        attn1(a)
                    if c == AT_QKV:
                        odds(a)
                        take_v(a, 0)
                    if c == AT_V23:
                        log_odds(a)
                        take_v(a, 1)
                    if c == AT_V23 + 1:
                        powers(a)
                    if c == AT_V23 + 2:
                        move_k(a)
                    if c == AT_SCORES:
                        attn3(a)
                    if c == AT_X2:
                        attn6(a)
                    if a < B and c >= NC - 4:
                        sines(a, (c - NC + 4) // 2, [c % 2])
                    if a == B and c == LT_X3:
                        attn8(B)
                if a == B:
                    break
                for k in range(NG):
                    if 2 <= k + 1 < NG:
                        sines(a, k + 1)
                    if k == TK_X3:
                        attn8(a)
                    if k == TK_LG:
                        router(a)
                    if k == TK_GT:
                        gates(a)
                take_h(a)
                if a == 2:
                    cls_silu(1)

            cls_silu(2)
            router(B)
            gates(B)
            for c in range(NC):
                silu(B - 1, c)

        @block.vector
        def _(dve):
            def layernorm(src, dst, a, which, TP, nt, done, twice=False, parts=(0, 1, 2)):
                n0 = (3 * a + which) * LNS
                step = [0 if 0 in parts else 2]

                def next_(ins):
                    step[0] += 1
                    ins.then_inc(ln_step, 1)
                    dve.wait_ge(ln_step, n0 + step[0])

                if 0 in parts:
                    for i in range(nt):
                        ins = dve.bn_stats(st[0:TP, i, :], src[0:TP, i, 0:D])
                    next_(ins)
                    for i in range(nt):
                        ins = dve.bn_aggr(mv[0:TP, i, :], st[0:TP, i, :])
                    next_(ins)
                v_, y_, a_ = ve[0:TP, 0:nt], y[0:TP, 0:nt], ya[0:TP, 0:nt]
                if 1 in parts:
                    next_(dve.tensor_scalar(v_, mv[0:TP, 0:nt, 1], LN_EPS, None, ALU.add))
                    next_(dve.tensor_scalar(y_.bitcast(I32), v_.bitcast(I32), 1, None, ALU.logical_shift_right))
                    next_(dve.tensor_scalar(y_.bitcast(I32), y_.bitcast(I32), -1.0, RSQRT_SEED, ALU.mult, ALU.add))
                    for _ in range(3):
                        next_(dve.scalar_tensor_tensor(a_, y_, -0.5, y_, ALU.mult, ALU.mult))
                        next_(dve.tensor_tensor(a_, a_, v_, ALU.mult))
                        next_(dve.scalar_tensor_tensor(y_, a_, 1.5, y_, ALU.add, ALU.mult))
                if 2 in parts:
                    for i in range(nt):
                        ins = dve.tensor_scalar(dst[0:TP, i, 0:D], src[0:TP, i, 0:D], mv[0:TP, i, 0:1],
                                                y[0:TP, i:i + 1], ALU.subtract, ALU.mult)
                        if twice:
                            ins = dve.tensor_scalar(dst[0:TP, i, D:D + DB], src[0:TP, i, P:D], mv[0:TP, i, 0:1],
                                                    y[0:TP, i:i + 1], ALU.subtract, ALU.mult)
                    ins.then_inc(done, 1)

            def remainders(a, k):
                q = NG * a + k
                s = k % SLOTS
                dve.wait_ge(n_ready, q + 1)
                for i in range(3):
                    fi = f_index(k, i)
                    ins = dve.scalar_tensor_tensor(feat[:, s, i, :], x[:, x_block(k), :], f_col[:, fi:fi + 1],
                                                   feat[:, s, i, :], ALU.mult, ALU.subtract)
                ins.then_inc(r_raw, 1)
                dve.wait_ge(r_raw, q + 1)
                dve.tensor_scalar(feat[:, s, 3:6, :].bitcast(I32), feat[:, s, 0:3, :].bitcast(I32), 0x7FFFFFFF, None,
                                  ALU.bitwise_and).then_inc(r_ready, 1)

            def attn0(a, parts=(0, 1, 2)):
                W, TP, nt = width(a)
                h_, _, xn_ = tiles(a)[:3]
                if a == 0:
                    dve.wait_ge(cls_in, 16)
                elif 0 in parts:
                    dve.wait_ge(h_ready, a)
                    dve.wait_ge(xpose3, a)
                layernorm(h_, xn_, a, 0, TP, nt, xn_ready, parts=parts)

            def attn1(a):
                W, TP, nt = width(a)
                dve.wait_ge(xpose1, a + 1)
                dve.tensor_copy(xt_b[:, 0:W], ps[0:DB, A1, 0:W]).then_inc(xtb_ready, 1)

            def negatives(a):
                W, TP, nt = width(a)
                dve.wait_ge(qk_psum, a + 1)
                dve.tensor_scalar(r[:, R_E, 0:W], ps[:, A2, 0:W], 0.0, None, ALU.min).then_inc(e_ready, 1)

            def clip_odds(a):
                W, TP, nt = width(a)
                dve.wait_ge(odds_ready, a + 1)
                dve.tensor_scalar(r[:, R_S, 0:W], r[:, R_S, 0:W], MAX_ODDS, None, ALU.min).then_inc(oddsc_ready, 1)
                dve.wait_ge(ee_ready, a + 1)
                dve.scalar_tensor_tensor(r[:, R_PHI, 0:W], ps[:, A2, 0:W], 0.0, r[:, R_E, 0:W],
                                         ALU.max, ALU.add).then_inc(phi_ready, 1)

            def running_sum(a):
                W, TP, nt = width(a)
                dve.wait_ge(s_ready, a + 1)
                dve.tensor_tensor_scan(r[:, R_C, 0:W], one[:, 0:1].to_broadcast([P, W]), r[:, R_S, 0:W],
                                       0.0 if a == 0 else s_c[:, 0:1], ALU.mult, ALU.add).then_inc(scan_ready, 1)
                dve.wait_ge(scan_ready, a + 1)
                if a == 0:
                    dve.tensor_copy(s_c[:, :], r[:, R_S, 0:1])
                dve.tensor_scalar(r[:, R_C, 0:W], r[:, R_C, 0:W], CLIP, -CLIP, ALU.min, ALU.max).then_inc(c_ready, 1)

            def weigh_qk(a):
                W, TP, nt = width(a)
                dve.wait_ge(p_ready, a + 1)
                dve.wait_ge(phi_ready, a + 1)
                dve.scalar_tensor_tensor(r[:, R_QK, 0:W], r[:, R_PHI, 0:W], qk_scale[:, 0:1], r[:, R_P, 0:W],
                                         ALU.mult, ALU.mult).then_inc(qk_ready, 1)

            def attn2(a):
                negatives(a)
                clip_odds(a)
                running_sum(a)
                weigh_qk(a)

            def attn3(a):
                W, TP, nt = width(a)
                dve.wait_ge(at_psum, a + 1)
                for j in range(nt):
                    bank, c0 = score_place(j)
                    ins = dve.tensor_tensor(at[0:TP, j, 0:TP], ps[0:TP, bank, c0:c0 + TP], causal[0:TP, 0:TP],
                                            ALU.mult)
                ins.then_inc(at_diag, 1)

            def make_state():
                dve.wait_ge(state_psum, 1)
                dve.tensor_scalar(state[:, :], ps[0:M, A1, 0:D + 1], r[0:M, R_K, 0:1], None,
                                  ALU.mult).then_inc(state_ready, 1)

            def divide(a):
                W, TP, nt = width(a)
                xn_ = tiles(a)[2]
                n = min(2, nt)
                dve.wait_ge(av_psum, a + 1)
                for i in range((nt + 1) // 2):
                    ins = dve.tensor_scalar(den[0:TP, 2 * i:2 * i + n], ps[0:TP, AV_BANK[i], 0:n * (D + 1)].rearrange(
                        "p (t d) -> p t d", d=D + 1)[:, :, D], DEN_EPS, None, ALU.add)
                ins.then_inc(den_ready, 1)
                dve.wait_ge(den_ready, a + 1)
                dve.reciprocal(rden[0:TP, 0:nt], den[0:TP, 0:nt]).then_inc(rden_ready, 1)
                dve.wait_ge(rden_ready, a + 1)
                for i in range(nt):
                    c0 = (i % 2) * (D + 1)
                    ins = dve.tensor_scalar(xn_[0:TP, i, 0:D], ps[0:TP, AV_BANK[i // 2], c0:c0 + D],
                                            rden[0:TP, i:i + 1], None, ALU.mult)
                ins.then_inc(hh_ready, 1)
                dve.wait_ge(hh_ready, a + 1)

            def norm_heads(a, parts=(0, 1, 2)):
                W, TP, nt = width(a)
                xn_ = tiles(a)[2]
                layernorm(xn_, xn_, a, 1, TP, nt, hn_ready, parts=parts)

            def attn5(a):
                divide(a)
                norm_heads(a)

            def attn6(a):
                W, TP, nt = width(a)
                dve.wait_ge(xpose2, a + 1)
                dve.tensor_scalar(xt_b[:, 0:W], ps[0:DB, A2, 0:W], gb_b[:, 0:1], gb_b[:, 1:2], ALU.mult,
                                  ALU.add).then_inc(ntb_ready, 1)

            def attn7(a, parts=(0, 1, 2)):
                W, TP, nt = width(a)
                h_, h2_, xn_ = tiles(a)[:3]
                dve.wait_ge(wo_psum, a + 1)
                if 2 <= a < B:
                    dve.wait_ge(out_dma, 16 * (a - 1))
                n = min(2, nt)
                for i in range((nt + 1) // 2):
                    ins = dve.tensor_tensor(
                        h2_[0:TP, 2 * i:2 * i + n, :], h_[0:TP, 2 * i:2 * i + n, :],
                        ps[0:TP, WO_BANK[i], 0:n * D].rearrange("p (t d) -> p t d", d=D), ALU.add)
                ins.then_inc(h2_ready, 1)
                dve.wait_ge(h2_ready, a + 1)
                norm_rest(a, parts)

            def norm_rest(a, parts):
                W, TP, nt = width(a)
                _, h2_, xn_ = tiles(a)[:3]
                layernorm(h2_, xn_, a, 2, TP, nt, xn2_ready, twice=True, parts=parts)

            def attn8(a):
                W, TP, nt = width(a)
                _, _, _, xh_a_, xl_a_, xh_b_, xl_b_, _ = tiles(a)
                dve.wait_ge(xh_ready, a + 1)
                dve.tensor_tensor(xl_a_[:, 0:W], ps[:, A2, 0:W], xh_a_[:, 0:W].bitcast(F32), ALU.subtract)
                dve.tensor_tensor(xl_b_[:, 0:W], ps[0:DB, A1, 0:W], xh_b_[0:DB, 0:W].bitcast(F32),
                                  ALU.subtract).then_inc(xl_ready, 1)

            TOPS = 12

            def router(a):
                W, TP, nt = width(a)
                step = [0]

                def next_(ins):
                    step[0] += 1
                    ins.then_inc(top_step, 1)
                    dve.wait_ge(top_step, TOPS * a + step[0])

                L, L2, K = lg[0:TP, 0:nt, 0:NE], lg2[0:TP, 0:nt, :], key[0:TP, 0:nt, :]
                ranks = rank[0:TP, :].unsqueeze(1).to_broadcast([TP, nt, NE])

                def wide(t):
                    return t.unsqueeze(2).to_broadcast([TP, nt, NE])

                dve.wait_ge(lg_psum, a + 1)
                next_(dve.tensor_copy(lg[0:TP, 0:nt, :], ps[0:TP, A0, 0:16 * nt].rearrange(
                    "p (t n) -> p t n", n=16)[:, :, 0:NE + 1]))
                for row, (src, oh) in enumerate(((L, oh1[0:TP, 0:nt, :]), (L2, oh2[0:TP, 0:nt, :]))):
                    best, at_ = top[0:TP, 2 * row, 0:nt], top[0:TP, 2 * row + 1, 0:nt]
                    next_(dve.tensor_reduce(best, src, AX_X, ALU.max))
                    next_(dve.tensor_tensor(K, src, wide(best), ALU.is_equal))
                    next_(dve.tensor_tensor(K, K, ranks, ALU.mult))
                    next_(dve.tensor_reduce(at_, K, AX_X, ALU.max))
                    next_(dve.tensor_tensor(oh, K, wide(at_), ALU.is_equal))
                    if row == 0:
                        next_(dve.scalar_tensor_tensor(L2, oh, -FAR, L, ALU.mult, ALU.add))
                assert step[0] == TOPS
                dve.tensor_tensor(dz[0:TP, 0:nt, 0], top[0:TP, 2, 0:nt], top[0:TP, 0, 0:nt], ALU.subtract)
                dve.tensor_scalar(dz[0:TP, 0:nt, 1], lg[0:TP, 0:nt, NE], sgb[0:TP, 0:1], -1.0, ALU.add,
                                  ALU.mult).then_inc(dz_ready, 1)
                dve.wait_ge(ez_ready, a + 1)
                gstep = [0]

                def gnext(ins):
                    gstep[0] += 1
                    ins.then_inc(gt_step, 1)
                    dve.wait_ge(gt_step, 8 * a + gstep[0])

                e, iz_ = ez[0:TP, 0:nt, :], iz[0:TP, 0:nt, :]
                gnext(dve.tensor_scalar(iz_, e, 1.0, None, ALU.add))
                gnext(dve.reciprocal(iz_, iz_))
                dve.tensor_tensor(ga[0:TP, 0:nt, 1], e[:, :, 0], iz_[:, :, 0], ALU.mult)
                gnext(dve.tensor_scalar(ga[0:TP, 0:nt, 2], iz_[:, :, 1], -1.0, 1.0, ALU.mult, ALU.add))
                dve.tensor_tensor(ga[0:TP, 0:nt, 0], iz_[:, :, 0], ga[0:TP, 0:nt, 2], ALU.mult)
                gnext(dve.tensor_tensor(ga[0:TP, 0:nt, 1], ga[0:TP, 0:nt, 1], ga[0:TP, 0:nt, 2], ALU.mult))
                dve.tensor_tensor(oh1[0:TP, 0:nt, :], oh1[0:TP, 0:nt, :], wide(ga[0:TP, 0:nt, 0]), ALU.mult)
                gnext(dve.tensor_tensor(oh2[0:TP, 0:nt, :], oh2[0:TP, 0:nt, :], wide(ga[0:TP, 0:nt, 1]), ALU.mult))
                dve.tensor_tensor(gm[0:TP, 0:nt, 0:NE], oh1[0:TP, 0:nt, :], oh2[0:TP, 0:nt, :], ALU.add)
                gnext(dve.tensor_copy(gm[0:TP, 0:nt, NE], iz_[:, :, 1]))
                gnext(dve.tensor_copy(gm_hi[0:TP, 0:nt, :], gm[0:TP, 0:nt, :]))
                dve.tensor_copy(gt[0:TP, 0:nt, 0:NE + 1], gm_hi[0:TP, 0:nt, :].bitcast(F32))
                gnext(dve.tensor_tensor(gt[0:TP, 0:nt, GLO:GR], gm[0:TP, 0:nt, :], gm_hi[0:TP, 0:nt, :].bitcast(F32),
                                        ALU.subtract))
                assert gstep[0] == 8

            def hidden(f, c):
                q = NC * f + c
                S_, t_, hid_ = fr[:, F_S + c % 2, :], fr[:, F_T, :], fr[:, F_H + c % 3, :]
                dve.wait_ge(u_psum, q + 1)
                dve.wait_ge(silu_ready, q + 1)
                if c >= 1:
                    dve.wait_ge(hid_ready, q)
                dve.tensor_tensor(t_, S_, ps[:, U0, :], ALU.mult).then_inc(t_ready, 1)
                dve.wait_ge(t_ready, q + 1)
                dve.wait_ge(m_psum, q + 1)
                if c >= 3:
                    dve.wait_ge(down_ready, q - 2)
                dve.tensor_tensor(hid_, t_, ps[:, M0, :], ALU.mult).then_inc(hid_ready, 1)

            def cls_hidden(n):
                um = ps[:, ROUND_BANKS[n][1], :]
                dve.wait_ge(umc_psum, n + 1)
                dve.wait_ge(siluc_ready, n + 1)
                dve.tensor_tensor(act_c[:, 1, :], act_c[:, 0, :], um[:, 0:CR * CLS], ALU.mult).then_inc(tc_ready, 1)
                dve.wait_ge(tc_ready, n + 1)
                dve.tensor_tensor(act_c[:, 2, :], act_c[:, 1, :], um[:, UM:UM + CR * CLS],
                                  ALU.mult).then_inc(hidc_ready, 1)

            def cls_finish(n):
                dve.wait_ge(downc_ready, n + 1)
                dve.tensor_tensor(h2_c[:, 0, :], h2_c[:, 0, :], ps[0:CLS, ROUND_BANKS[n][2], 0:D],
                                  ALU.add).then_inc(outc_ready, 1)

            def finish(f):
                dve.wait_ge(down_ready, NC * (f + 1))
                h2_ = tiles(f + 1)[1]
                for i in range(2):
                    ins = dve.tensor_tensor(
                        h2_[:, 2 * i:2 * i + 2, :], h2_[:, 2 * i:2 * i + 2, :],
                        ps[:, DN0 + i, 0:2 * D].rearrange("p (t d) -> p t d", d=D), ALU.add)
                ins.then_inc(out_ready, 1)

            def split_piece(p):
                cut = slice(PC * p, PC * (p + 1))
                dve.wait_ge(split_hi, 2 * p + 2)
                dve.tensor_tensor(wa_lo[:, cut, :, :].rearrange("p c t n -> p (c t n)"),
                                  h2[:, :, :].rearrange("p a b -> p (a b)"),
                                  wa_hi[:, cut, :, :].rearrange("p c t n -> p (c t n)").bitcast(F32),
                                  ALU.subtract).then_inc(split_done, 1)
                low = wb[DB:P, cut, :, :].rearrange("p c t n -> p (c t n)")
                dve.tensor_tensor(low, xn[DB:P, :, :].rearrange("p a b -> p (a b)")[:, 0:PC * 2 * P], low.bitcast(F32),
                                  ALU.subtract).then_inc(split_done, 1)

            dve.memset(half_pi[:, :], HALF_PI).then_inc(consts_ok, 1)
            dve.memset(one[:, :], 1.0)
            dve.memset(v[:, :, D:D + 1], 1.0)
            dve.memset(gt[:, :, :], 0.0)
            dve.memset(qk_scale[0:M, :], float(M) ** -0.5)
            dve.memset(qk_scale[M:P, :], 1.0)
            dve.memset(p_sign[0:M, :], -1.0)
            dve.memset(p_sign[M:P, :], 1.0)
            remainders(0, 0)
            remainders(0, 1)
            attn0(0)
            dve.wait_ge(w_small, 16)
            dve.tensor_scalar(neg_bf, neg_bf, -1.0, None, ALU.mult)
            dve.tensor_copy(pick[:, :, :], pick_raw.unsqueeze(2).to_broadcast([GR, NE + 1, P // 2])).then_inc(consts_ok, 1)
            remainders(0, 2)
            attn1(0)
            dve.tensor_copy(wra_hi[:, :], wr_raw[:, 0, :])
            dve.tensor_copy(wrb[:, :], wr_raw[:, 1, :]).then_inc(router_split, 1)
            dve.wait_ge(router_split, 1)
            dve.tensor_tensor(wra_lo[:, :], wr_raw[:, 0, :], wra_hi[:, :].bitcast(F32), ALU.subtract)
            dve.tensor_tensor(wrb[DB:P, :], wr_raw[DB:P, 1, :], wrb[DB:P, :].bitcast(F32),
                              ALU.subtract).then_inc(router_split, 1)
            remainders(0, 3)
            attn2(0)
            remainders(0, 4)
            attn3(0)
            make_state()
            attn5(0)
            split_piece(0)
            remainders(0, 5)
            attn6(0)
            split_piece(1)
            remainders(0, 6)
            attn7(0)
            split_piece(2)
            remainders(0, 7)
            attn8(0)
            split_piece(3)
            remainders(0, 8)
            router(0)
            split_piece(4)
            remainders(1, 0)
            split_piece(5)
            remainders(1, 1)

            dve.wait_ge(split_done, 2 * PIECES)
            attn0(1)
            remainders(1, 2)
            attn1(1)
            remainders(1, 3)
            negatives(1)
            clip_odds(1)
            remainders(1, 4)
            running_sum(1)
            weigh_qk(1)
            remainders(1, 5)
            attn3(1)
            remainders(1, 6)
            attn5(1)
            remainders(1, 7)
            attn6(1)
            remainders(1, 8)
            attn7(1)
            attn8(1)
            router(1)
            attn0(2, [0])
            cls_hidden(0)

            for a in range(2, B + 1):
                if a > 2:
                    attn0(a, [0])
                if a == 3:
                    cls_hidden(1)
                for c in range(NC):
                    hidden(a - 2, c)
                    if c == 0:
                        attn0(a, [1])
                    if c == 1:
                        attn0(a, [2])
                        if a < B:
                            cls_finish(a - 2)
                    if c == AT_X1:
                        attn1(a)
                    if c == AT_QKV:
                        negatives(a)
                    if c == AT_V23:
                        clip_odds(a)
                    if c == AT_V23 + 1:
                        running_sum(a)
                    if c == AT_V23 + 2:
                        weigh_qk(a)
                    if c == AT_SCORES:
                        attn3(a)
                    if c == AT_AV:
                        divide(a)
                        norm_heads(a, [0])
                    if c in (AT_AV + 1, AT_AV + 2):
                        norm_heads(a, [c - AT_AV])
                    if c == AT_X2:
                        attn6(a)
                    if a < B and c in AT_AHEAD:
                        remainders(a, AT_AHEAD.index(c))
                    if a == B and c == LT_WO:
                        attn7(B, [0])
                    if a == B and c in (LT_WO + 1, LT_WO + 2):
                        norm_rest(B, [c - LT_WO])
                    if a == B and c == LT_X3:
                        attn8(B)
                finish(a - 2)
                if a == B:
                    break
                for k in range(NG):
                    if k + 2 < NG:
                        remainders(a, k + 2)
                    if k == TK_WO:
                        attn7(a)
                    if k == TK_X3:
                        attn8(a)
                    if k == TK_LG:
                        router(a)

            router(B)
            cls_hidden(2)
            cls_finish(2)
            for c in range(NC):
                hidden(B - 1, c)
            finish(B - 1)

        @block.tensor
        def _(pe):
            def project(a, k):
                q = NG * a + k
                if a == 0:
                    pe.wait_ge(wt_in[k], x_parts(k))
                elif k == 0:
                    pe.wait_ge(h_ready, a)
                if k == 0 and a >= 2:
                    pe.wait_ge(silu_ready, NC * (a - 1))
                    pe.wait_ge(t_ready, NC * (a - 1))
                for i in range(6):
                    if i % 3 == 0:
                        pe.wait_ge(sin_ready, 2 * q + 1 + i // 3)
                    for t in range(NT):
                        ins = pe.matmul(ps[:, TB0 + t // 2, (t % 2) * D:(t % 2 + 1) * D],
                                        feat[:, k % SLOTS, i, t * P:(t + 1) * P], w_tok[:, k, i, :],
                                        start=(k == 0 and i == 0 and t % 2 == 0), stop=(k == NG - 1 and i == 5),
                                        skip_group_check=True)
                ins.then_inc(tok_group, 1)

            def attn1(a):
                W, TP, nt = width(a)
                xn_ = tiles(a)[2]
                pe.wait_ge(xn_ready, a + 1)
                for i in range(nt):
                    pe.transpose(ps[:, A0, i * P:i * P + TP], xn_[0:TP, i, 0:P], ident[0:TP, 0:TP])
                for i in range(nt):
                    ins = pe.transpose(ps[0:DB, A1, i * P:i * P + TP], xn_[0:TP, i, P:D], ident[0:TP, 0:TP])
                ins.then_inc(xpose1, 1)

            def values(a, first):
                W, TP, nt = width(a)
                for i in range(first, min(first + 2, nt)):
                    o = ps[0:TP, (A1, A0)[i // 2], (i % 2) * D:(i % 2 + 1) * D]
                    pe.matmul(o, xt_a[:, i * P:i * P + TP], wv_a[:, :], start=True, stop=False)
                    ins = pe.matmul(o, xt_b[:, i * P:i * P + TP], wv_b[:, :], start=False, stop=True)
                ins.then_inc((v01_psum, v23_psum)[first // 2], 1)

            def attn2(a):
                W, TP, nt = width(a)
                pe.wait_ge(xta_ready, a + 1)
                pe.wait_ge(xtb_ready, a + 1)

                def pair(bank, wa, wb_):
                    pe.matmul(ps[:, bank, 0:W], wa, xt_a[:, 0:W], start=True, stop=False)
                    return pe.matmul(ps[:, bank, 0:W], wb_, xt_b[:, 0:W],
                                     start=False, stop=True)

                pair(A0, wff_a, wff_b).then_inc(f_psum, 1)
                if a >= 1:
                    pe.wait_ge(gate_ready, a)
                pair(A2, wqk_a, wqk_b).then_inc(qk_psum, 1)
                values(a, 0)

            def attn2b(a):
                pe.wait_ge(odds_ready, a + 1)
                values(a, 2)

            def attn3(a):
                W, TP, nt = width(a)
                pe.wait_ge(k_in, 16 * (a + 1))
                pe.wait_ge(qk_ready, a + 1)
                pe.wait_ge(v_ready, a + 1)
                for j in range(nt):
                    bank, c0 = score_place(j)
                    ins = pe.matmul(ps[0:TP, bank, c0:c0 + W - P * j], r[0:M, R_K, j * P:j * P + TP],
                                    r[0:M, R_QK, j * P:W], start=True, stop=True)
                ins.then_inc(at_psum, 1)

            def attn5(a):
                W, TP, nt = width(a)
                if a == 0:
                    pe.matmul(ps[0:M, A1, 0:D + 1], causal[0:1, 0:M], v[0:1, 0, :], start=True,
                              stop=True).then_inc(state_psum, 1)
                pe.wait_ge(at_diag, a + 1)
                if a >= 1:
                    pe.wait_ge(at_rest, a)
                    pe.wait_ge(state_ready, 1)
                for i in range(nt):
                    o = ps[0:TP, AV_BANK[i // 2], (i % 2) * (D + 1):(i % 2 + 1) * (D + 1)]
                    if a >= 1:
                        pe.matmul(o, r[0:M, R_QK, i * P:(i + 1) * P], state[:, :], start=(i % 2 == 0), stop=False,
                                  skip_group_check=True)
                    for j in range(i + 1):
                        ins = pe.matmul(o, at[0:TP, j, (i - j) * P:(i - j) * P + TP], v[0:TP, j, :],
                                        start=(nt == 1), stop=(j == i), skip_group_check=True)
                ins.then_inc(av_psum, 1)

            def attn6(a):
                W, TP, nt = width(a)
                xn_ = tiles(a)[2]
                pe.wait_ge(hn_ready, a + 1)
                for i in range(nt):
                    pe.transpose(ps[:, A0, i * P:i * P + TP], xn_[0:TP, i, 0:P], ident[0:TP, 0:TP])
                for i in range(nt):
                    ins = pe.transpose(ps[0:DB, A2, i * P:i * P + TP], xn_[0:TP, i, P:D], ident[0:TP, 0:TP])
                ins.then_inc(xpose2, 1)

            def attn7(a):
                W, TP, nt = width(a)
                pe.wait_ge(nta_ready, a + 1)
                pe.wait_ge(ntb_ready, a + 1)
                for i in range(nt):
                    o = ps[0:TP, WO_BANK[i // 2], (i % 2) * D:(i % 2 + 1) * D]
                    pe.matmul(o, xt_a[:, i * P:i * P + TP], wo_a[:, :], start=True, stop=False)
                    ins = pe.matmul(o, xt_b[:, i * P:i * P + TP], wo_b[:, :], start=False, stop=True)
                ins.then_inc(wo_psum, 1)

            def attn8(a):
                W, TP, nt = width(a)
                xn_ = tiles(a)[2]
                pe.wait_ge(xn2_ready, a + 1)
                for i in range(nt):
                    pe.transpose(ps[:, A2, i * P:i * P + TP], xn_[0:TP, i, 0:P], ident[0:TP, 0:TP])
                for i in range(nt):
                    ins = pe.transpose(ps[:, A1, i * P:i * P + TP], xn_[0:TP, i, P:D + DB], ident[0:TP, 0:TP])
                ins.then_inc(xpose3, 1)

            def router(a):
                W, TP, nt = width(a)
                _, _, _, xh_a_, xl_a_, xh_b_, xl_b_, _ = tiles(a)
                pe.wait_ge(xh_ready, a + 1)
                pe.wait_ge(xl_ready, a + 1)
                for i in range(nt):
                    o, c = ps[0:TP, A0, 16 * i:16 * i + NR], slice(i * P, i * P + TP)
                    pe.matmul(o, xh_a_[:, c], wra_hi[:, :], start=True, stop=False)
                    pe.matmul(o, xh_a_[:, c], wra_lo[:, :], start=False, stop=False)
                    pe.matmul(o, xl_a_[:, c], wra_hi[:, :], start=False, stop=False)
                    pe.matmul(o, xh_b_[:, c], wrb[:, :], start=False, stop=False)
                    ins = pe.matmul(o, xl_b_[:, c], wrb[0:DB, :], start=False, stop=True)
                ins.then_inc(lg_psum, 1)

            def gates(a):
                W, TP, nt = width(a)
                pe.wait_ge(gt_step, 8 * (a + 1))
                for i in range(nt):
                    ins = pe.transpose(ps[0:GR, A2, i * P:i * P + TP], gt[0:TP, i, :], ident[0:TP, 0:TP])
                ins.then_inc(gt_psum, 1)

            def product(o, c, i, xh, xl, yh, yl):
                pe.matmul(o, wa_hi[:, c, i, :], xh, start=True, stop=False)
                pe.matmul(o, wa_lo[:, c, i, :], xh, start=False, stop=False)
                pe.matmul(o, wa_hi[:, c, i, :], xl, start=False, stop=False)
                pe.matmul(o, wb[:, c, i, :], yh, start=False, stop=False)
                return pe.matmul(o, wb[0:DB, c, i, :], yl, start=False, stop=True)

            def unit_gates(o, c, gate_):
                e0 = NE if c < NCS else (c - NCS) * P // D
                e1 = NE if c < NCS else ((c - NCS) * P + P - 1) // D
                sel = (pick[:, e0, 0:1].to_broadcast([GR, P]) if e0 == e1 else
                       pick[:, e0:e0 + 2, :].rearrange("k e m -> k (e m)"))
                return pe.matmul(o, sel, gate_, start=True, stop=True)

            def up(f, c):
                q = NC * f + c
                _, _, _, *operands, gate_ = tiles(f + 1)
                operands = [x_[:, :] for x_ in operands]
                for i, (bank, done, read) in enumerate(((G0, g_psum, silu_ready), (U0, u_psum, t_ready))):
                    if q >= 1:
                        pe.wait_ge(read, q)
                    product(ps[:, bank, :], c, i, *operands).then_inc(done, 1)
                if q >= 1:
                    pe.wait_ge(hid_ready, q)
                unit_gates(ps[:, M0, :], c, gate_[:, :]).then_inc(m_psum, 1)

            def down(f, c):
                q = NC * f + c
                pe.wait_ge(hid_ready, q + 1)
                if c == 0 and f >= 1:
                    pe.wait_ge(out_ready, f)
                for t in range(NT):
                    ins = pe.matmul(ps[:, DN0 + t // 2, (t % 2) * D:(t % 2 + 1) * D],
                                    fr[:, F_H + c % 3, t * P:(t + 1) * P], w_down[:, c, :],
                                    start=(c == 0 and t % 2 == 0), stop=(c == NC - 1), skip_group_check=True)
                ins.then_inc(down_ready, 1)

            def ffn_step(f, c):
                if c < NC:
                    up(f, c)
                if c >= 1:
                    down(f, c - 1)

            def cls_up(n):
                g_bank, um_bank, _ = ROUND_BANKS[n]
                operands = [x_[:, :] for x_ in (xhc_a, xlc_a, xhc_b, xlc_b)]
                for j in range(CR):
                    ins = product(ps[:, g_bank, CLS * j:CLS * (j + 1)], CR * n + j, 0, *operands)
                ins.then_inc(gc_psum, 1)
                for j in range(CR):
                    product(ps[:, um_bank, CLS * j:CLS * (j + 1)], CR * n + j, 1, *operands)
                for j in range(CR):
                    ins = unit_gates(ps[:, um_bank, UM + CLS * j:UM + CLS * (j + 1)], CR * n + j, gatec_t[:, :])
                ins.then_inc(umc_psum, 1)

            def cls_down(n):
                pe.wait_ge(hidc_ready, n + 1)
                for j in range(CR):
                    ins = pe.matmul(ps[0:CLS, ROUND_BANKS[n][2], 0:D], act_c[:, 2, CLS * j:CLS * (j + 1)],
                                    w_down[:, CR * n + j, :], start=(j == 0), stop=(j == CR - 1))
                ins.then_inc(downc_ready, 1)

            project(0, 0)
            project(0, 1)
            pe.wait_ge(w_small, 16)
            attn1(0)
            project(0, 2)
            pe.wait_ge(consts_ok, 2)
            attn2(0)
            project(0, 3)
            attn3(0)
            attn5(0)
            project(0, 4)
            attn6(0)
            project(0, 5)
            attn7(0)
            project(0, 6)
            attn8(0)
            project(0, 7)
            pe.wait_ge(router_split, 2)
            router(0)
            project(0, 8)
            gates(0)

            project(1, 0)
            attn1(1)
            project(1, 1)
            attn2(1)
            project(1, 2)
            attn2b(1)
            project(1, 3)
            attn3(1)
            project(1, 4)
            attn5(1)
            project(1, 5)
            attn6(1)
            project(1, 6)
            attn7(1)
            project(1, 7)
            attn8(1)
            project(1, 8)
            router(1)
            pe.wait_ge(split_done, 2 * PIECES)
            pe.wait_ge(wdown_in, 16)
            gates(1)
            cls_up(0)

            for a in range(2, B + 1):
                pe.wait_ge(h_ready, a)
                pe.wait_ge(gate_ready, a)
                for c in range(NC + 1):
                    if c < NC:
                        up(a - 2, c)
                    if c == 1 and a < B:
                        cls_down(a - 2)
                    if c == AT_X1:
                        attn1(a)
                    if c == AT_QKV:
                        if a < B:
                            pe.wait_ge(outc_ready, a - 1)
                        attn2(a)
                    if c == AT_V23:
                        attn2b(a)
                    if c == AT_SCORES:
                        attn3(a)
                    if c == AT_AV:
                        attn5(a)
                    if c == AT_X2:
                        attn6(a)
                    if a == B and c == LT_WO:
                        attn7(B)
                    if a == B and c == LT_X3:
                        attn8(B)
                    if a == B and c == LT_LG:
                        router(B)
                    if c >= 1:
                        down(a - 2, c - 1)
                if a == B:
                    break
                for k in range(NG):
                    if k == TK_WO:
                        attn7(a)
                    if k == TK_X3:
                        attn8(a)
                    if k == TK_LG:
                        router(a)
                    if k == TK_GT:
                        gates(a)
                    project(a, k)
                if a == 2:
                    cls_up(1)

            pe.wait_ge(silu_ready, NC * (B - 1))
            pe.wait_ge(t_ready, NC * (B - 1))
            cls_up(2)
            gates(B)
            cls_down(2)
            pe.wait_ge(gate_ready, B + 1)
            pe.wait_ge(siluc_ready, 3)
            for c in range(NC + 1):
                ffn_step(B - 1, c)


def kernel(x, cls_tok, L0_tok_freq_bands, L0_tok_W, L0_attn_Wq, L0_attn_Wk, L0_attn_Wv, L0_attn_Wf, L0_attn_bf,
           L0_attn_Wo, L0_attn_gamma, L0_attn_beta, L0_ffn_router_w, L0_ffn_w_gate, L0_ffn_w_up, L0_ffn_w_down,
           L0_ffn_ws_gate, L0_ffn_ws_up, L0_ffn_ws_down, L0_ffn_sg_w, L0_ffn_sg_b):
    import concourse.bacc as bacc
    from concourse.bass_utils import run_bass_kernel_spmd

    def experts(w):
        return np.asarray(w).transpose(1, 0, 2).reshape(D, NE * D)

    gate = np.concatenate([np.asarray(L0_ffn_ws_gate), experts(L0_ffn_w_gate)], axis=1)
    up = np.concatenate([np.asarray(L0_ffn_ws_up), experts(L0_ffn_w_up)], axis=1)
    packed = np.zeros((P, PACKED), np.float32)

    def put(name, rows, lo=0):
        c0, n = PACK[name]
        rows = np.asarray(rows)
        packed[lo:lo + rows.shape[0], c0:c0 + n] = rows

    qk = np.concatenate([np.asarray(L0_attn_Wq), np.asarray(L0_attn_Wk)], axis=1)
    ff = np.tile(np.asarray(L0_attn_Wf), (1, 2))
    for name, w in (("qk", qk), ("ff", ff), ("v", np.asarray(L0_attn_Wv)), ("o", np.asarray(L0_attn_Wo))):
        put(name + "_a", w[0:P])
        put(name + "_b", w[P:D], DB)
    put("neg_bf", np.tile(np.asarray(L0_attn_bf), 2).reshape(P, 1))
    gb = np.stack([np.asarray(L0_attn_gamma), np.asarray(L0_attn_beta)], axis=1)
    put("gb_a", gb[0:P])
    put("gb_b", gb[P:D])
    wr = np.zeros((D, NR), np.float32)
    wr[:, 0:NE], wr[:, NE:NE + 1] = np.asarray(L0_ffn_router_w), np.asarray(L0_ffn_sg_w)
    put("wr", np.concatenate([wr[0:P], np.concatenate([wr[P:D], wr[P:D]], axis=0)], axis=1))
    put("sgb", np.broadcast_to(np.asarray(L0_ffn_sg_b).reshape(1, 1), (P, 1)))
    put("ident", np.eye(P, dtype=np.float32))
    put("causal", np.triu(np.ones((P, P), np.float32)))
    for row in (0, GLO):
        put("pick", np.eye(NE + 1, dtype=np.float32), row)
    put("rank", np.broadcast_to(np.arange(NE, 0, -1, dtype=np.float32), (P, NE)))
    fr = np.asarray(L0_tok_freq_bands)
    arrays = {
        "xT": np.asarray(x).reshape(B, T, J).transpose(0, 2, 1),
        "wT": np.asarray(L0_tok_W).reshape(D, J, 2 * NF).transpose(1, 2, 0),
        "freqs": np.stack([np.concatenate([fr, fr[half::2]]) for half in range(2)]),
        "cls_tok": np.asarray(cls_tok).reshape(1, D),
        "packed": packed,
        "wgu": np.stack([gate.reshape(D, NC, P), up.reshape(D, NC, P)], axis=2).reshape(D, NC, 2 * P),
        "wd": np.concatenate([np.asarray(L0_ffn_ws_down), np.asarray(L0_ffn_w_down).reshape(NE * D, D)], axis=0),
    }
    arrays = {n: np.ascontiguousarray(a) for n, a in arrays.items()}
    nc = bacc.Bacc("TRN2", target_bir_lowering=False, num_devices=1)
    args = [nc.dram_tensor(f"in_{n}", a.shape, mybir.dt.from_np(a.dtype), kind="ExternalInput").ap()
            for n, a in arrays.items()]
    out = nc.dram_tensor("out", (B, T + 1, D), F32, kind="ExternalOutput").ap()
    build(nc, *args, out)
    res = run_bass_kernel_spmd(nc, [{f"in_{n}": a for n, a in arrays.items()}], core_ids=[0])
    return res.results[0]["out"]
```
